# Optimizing a Trainium2 kernel written in Bass

```python
import numpy as np
import jax
import jax.numpy as jnp

def _softmax(x, axis=-1):
    return jax.nn.softmax(x, axis=axis)

def _gelu(x):
    return jax.nn.gelu(x, approximate=True)

def _silu(x):
    return jax.nn.silu(x)

def _sigmoid(x):
    return jax.nn.sigmoid(x)

def _layernorm(x, axis=-1, eps=1e-05):
    m = jnp.mean(x, axis=axis, keepdims=True)
    v = jnp.var(x, axis=axis, keepdims=True)
    return (x - m) / jnp.sqrt(v + eps)

def _scatter_add(tgt, idx, src, axis=0):
    return tgt.at[idx].add(src)

def _segment_sum(src, seg, n):
    return jax.ops.segment_sum(src, seg, n)
kernel_name = 'mk_macaron_d1_jaxref_r4_7fba70'

def setup_inputs(seed: int=0):
    np.random.seed(seed)
    _w = jnp.asarray

    def _L0_attn_setup():
        import jax, jax.numpy as jnp
        import numpy as np
        B, T, C = (8, 512, 256)
        HID = 4 * C
        EPS = 1e-05

        def layernorm(x, g, b):
            m = jnp.mean(x, axis=-1, keepdims=True)
            v = jnp.mean(jnp.square(x - m), axis=-1, keepdims=True)
            return (x - m) * jax.lax.rsqrt(v + EPS) * g + b

        def time_shift(x):
            return jnp.concatenate([jnp.zeros_like(x[:, :1]), x[:, :-1]], axis=1)

        def wkv(time_decay, time_first, k, v):
            w = -jnp.exp(time_decay)
            u = time_first
            kT = jnp.swapaxes(k, 0, 1)
            vT = jnp.swapaxes(v, 0, 1)

            def step(carry, kv):
                aa, bb, pp = carry
                kt, vt = kv
                ww = u + kt
                p = jnp.maximum(pp, ww)
                e1 = jnp.exp(pp - p)
                e2 = jnp.exp(ww - p)
                y = (e1 * aa + e2 * vt) / (e1 * bb + e2)
                ww2 = pp + w
                p2 = jnp.maximum(ww2, kt)
                e1b = jnp.exp(ww2 - p2)
                e2b = jnp.exp(kt - p2)
                return ((e1b * aa + e2b * vt, e1b * bb + e2b, p2), y)
            init = (jnp.zeros((k.shape[0], k.shape[2]), k.dtype), jnp.zeros((k.shape[0], k.shape[2]), k.dtype), jnp.full((k.shape[0], k.shape[2]), -1e+38, k.dtype))
            _, ys = jax.lax.scan(step, init, (kT, vT))
            return jnp.swapaxes(ys, 0, 1)
        key = jax.random.key(seed)
        ks = jax.random.split(key, 24)
        s = 0.02
        d = {'x': jax.random.normal(ks[0], (B, T, C), jnp.float32), 'ln1_g': jnp.ones((C,), jnp.float32), 'ln1_b': jnp.zeros((C,), jnp.float32), 'ln2_g': jnp.ones((C,), jnp.float32), 'ln2_b': jnp.zeros((C,), jnp.float32), 'time_decay': jax.random.normal(ks[1], (C,), jnp.float32) - 2.0, 'time_first': jax.random.normal(ks[2], (C,), jnp.float32) * 0.5 + np.log(0.3).astype(np.float32), 'tm_k': jax.random.uniform(ks[3], (1, 1, C), jnp.float32), 'tm_v': jax.random.uniform(ks[4], (1, 1, C), jnp.float32), 'tm_r': jax.random.uniform(ks[5], (1, 1, C), jnp.float32), 'Wk': jax.random.normal(ks[6], (C, C), jnp.float32) * s, 'Wv': jax.random.normal(ks[7], (C, C), jnp.float32) * s, 'Wr': jax.random.normal(ks[8], (C, C), jnp.float32) * s, 'Wo': jax.random.normal(ks[9], (C, C), jnp.float32) * s, 'cm_k': jax.random.uniform(ks[10], (1, 1, C), jnp.float32), 'cm_r': jax.random.uniform(ks[11], (1, 1, C), jnp.float32), 'Wck': jax.random.normal(ks[12], (HID, C), jnp.float32) * s, 'Wcr': jax.random.normal(ks[13], (C, C), jnp.float32) * s, 'Wcv': jax.random.normal(ks[14], (C, HID), jnp.float32) * s}
        return d
    _L0_attn_in = _L0_attn_setup()

    def _L0_ffn_setup():
        import jax, jax.numpy as jnp
        import numpy as np
        key = jax.random.key(seed)
        k_x, k_W, k_b, k_ids, k_w = jax.random.split(key, 5)
        N_ADAPTERS, D_OUT, D_IN = (32, 256, 256)
        B, S = (2, 512)
        K = 8
        x = jax.random.normal(k_x, (B, S, D_IN), dtype=jnp.float32)
        W = jax.random.normal(k_W, (N_ADAPTERS, D_OUT, D_IN), dtype=jnp.float32)
        b = jax.random.normal(k_b, (N_ADAPTERS, D_OUT), dtype=jnp.float32)
        ids = jax.random.randint(k_ids, (K,), 0, N_ADAPTERS, dtype=jnp.int64)
        weights = jax.random.uniform(k_w, (K,), dtype=jnp.float32)
        return {'x': x, 'W': W, 'b': b, 'ids': ids, 'weights': weights}
    _L0_ffn_in = _L0_ffn_setup()
    _d = {'L0_attn_x': _L0_attn_in['x'], 'L0_attn_ln1_g': _L0_attn_in['ln1_g'], 'L0_attn_ln1_b': _L0_attn_in['ln1_b'], 'L0_attn_ln2_g': _L0_attn_in['ln2_g'], 'L0_attn_ln2_b': _L0_attn_in['ln2_b'], 'L0_attn_time_decay': _L0_attn_in['time_decay'], 'L0_attn_time_first': _L0_attn_in['time_first'], 'L0_attn_tm_k': _L0_attn_in['tm_k'], 'L0_attn_tm_v': _L0_attn_in['tm_v'], 'L0_attn_tm_r': _L0_attn_in['tm_r'], 'L0_attn_Wk': _L0_attn_in['Wk'], 'L0_attn_Wv': _L0_attn_in['Wv'], 'L0_attn_Wr': _L0_attn_in['Wr'], 'L0_attn_Wo': _L0_attn_in['Wo'], 'L0_attn_cm_k': _L0_attn_in['cm_k'], 'L0_attn_cm_r': _L0_attn_in['cm_r'], 'L0_attn_Wck': _L0_attn_in['Wck'], 'L0_attn_Wcr': _L0_attn_in['Wcr'], 'L0_attn_Wcv': _L0_attn_in['Wcv'], 'L0_ffn_W': _L0_ffn_in['W'], 'L0_ffn_b': _L0_ffn_in['b'], 'L0_ffn_ids': _L0_ffn_in['ids'], 'L0_ffn_weights': _L0_ffn_in['weights']}
    _x0 = _d['L0_attn_x']
    _d['L0_attn_x'] = jax.random.normal(jax.random.fold_in(jax.random.key(seed), 1), (8, 512, 256), dtype=_x0.dtype)
    del _x0
    return _d

def reference(L0_attn_x, L0_attn_ln1_g, L0_attn_ln1_b, L0_attn_ln2_g, L0_attn_ln2_b, L0_attn_time_decay, L0_attn_time_first, L0_attn_tm_k, L0_attn_tm_v, L0_attn_tm_r, L0_attn_Wk, L0_attn_Wv, L0_attn_Wr, L0_attn_Wo, L0_attn_cm_k, L0_attn_cm_r, L0_attn_Wck, L0_attn_Wcr, L0_attn_Wcv, L0_ffn_W, L0_ffn_b, L0_ffn_ids, L0_ffn_weights):

    def _L0_attn_ref(x, ln1_g, ln1_b, ln2_g, ln2_b, time_decay, time_first, tm_k, tm_v, tm_r, Wk, Wv, Wr, Wo, cm_k, cm_r, Wck, Wcr, Wcv):
        import jax, jax.numpy as jnp
        import numpy as np
        B, T, C = (8, 512, 256)
        HID = 4 * C
        EPS = 1e-05

        def layernorm(x, g, b):
            m = jnp.mean(x, axis=-1, keepdims=True)
            v = jnp.mean(jnp.square(x - m), axis=-1, keepdims=True)
            return (x - m) * jax.lax.rsqrt(v + EPS) * g + b

        def time_shift(x):
            return jnp.concatenate([jnp.zeros_like(x[:, :1]), x[:, :-1]], axis=1)

        def wkv(time_decay, time_first, k, v):
            w = -jnp.exp(time_decay)
            u = time_first
            kT = jnp.swapaxes(k, 0, 1)
            vT = jnp.swapaxes(v, 0, 1)

            def step(carry, kv):
                aa, bb, pp = carry
                kt, vt = kv
                ww = u + kt
                p = jnp.maximum(pp, ww)
                e1 = jnp.exp(pp - p)
                e2 = jnp.exp(ww - p)
                y = (e1 * aa + e2 * vt) / (e1 * bb + e2)
                ww2 = pp + w
                p2 = jnp.maximum(ww2, kt)
                e1b = jnp.exp(ww2 - p2)
                e2b = jnp.exp(kt - p2)
                return ((e1b * aa + e2b * vt, e1b * bb + e2b, p2), y)
            init = (jnp.zeros((k.shape[0], k.shape[2]), k.dtype), jnp.zeros((k.shape[0], k.shape[2]), k.dtype), jnp.full((k.shape[0], k.shape[2]), -1e+38, k.dtype))
            _, ys = jax.lax.scan(step, init, (kT, vT))
            return jnp.swapaxes(ys, 0, 1)
        h = layernorm(x, ln1_g, ln1_b)
        hh = time_shift(h)
        xk = h * tm_k + hh * (1 - tm_k)
        xv = h * tm_v + hh * (1 - tm_v)
        xr = h * tm_r + hh * (1 - tm_r)
        k = jnp.einsum('btc,oc->bto', xk, Wk)
        v = jnp.einsum('btc,oc->bto', xv, Wv)
        sr = jax.nn.sigmoid(jnp.einsum('btc,oc->bto', xr, Wr))
        rwkv = sr * wkv(time_decay, time_first, k, v)
        x = x + jnp.einsum('btc,oc->bto', rwkv, Wo)
        h = layernorm(x, ln2_g, ln2_b)
        hh = time_shift(h)
        xk = h * cm_k + hh * (1 - cm_k)
        xr = h * cm_r + hh * (1 - cm_r)
        kk = jnp.einsum('btc,hc->bth', xk, Wck)
        kk = jnp.square(jax.nn.relu(kk))
        kv = jnp.einsum('bth,ch->btc', kk, Wcv)
        rkv = jax.nn.sigmoid(jnp.einsum('btc,oc->bto', xr, Wcr)) * kv
        return x + rkv

    def _L0_ffn_ref(x, W, b, ids, weights):
        import jax, jax.numpy as jnp
        import numpy as np
        Wsel = W[ids]
        bsel = b[ids]
        out = jnp.einsum('k,kod,bsd->bso', weights, Wsel, x)
        out = out + jnp.einsum('k,ko->o', weights, bsel)
        return out
    x = L0_attn_x
    x = x + 0.5 * _L0_ffn_ref(_layernorm(x, axis=-1), L0_ffn_W, L0_ffn_b, L0_ffn_ids, L0_ffn_weights)
    x = x + _L0_attn_ref(_layernorm(x, axis=-1), L0_attn_ln1_g, L0_attn_ln1_b, L0_attn_ln2_g, L0_attn_ln2_b, L0_attn_time_decay, L0_attn_time_first, L0_attn_tm_k, L0_attn_tm_v, L0_attn_tm_r, L0_attn_Wk, L0_attn_Wv, L0_attn_Wr, L0_attn_Wo, L0_attn_cm_k, L0_attn_cm_r, L0_attn_Wck, L0_attn_Wcr, L0_attn_Wcv)
    x = x + 0.5 * _L0_ffn_ref(_layernorm(x, axis=-1), L0_ffn_W, L0_ffn_b, L0_ffn_ids, L0_ffn_weights)
    return x

_drawn_inputs = setup_inputs


def setup_inputs(seed=0):
    import zlib

    import numpy as np

    out = dict(_drawn_inputs(seed))
    spreads = {'L0_attn_ln1_g': (1.0, 0.6),
     'L0_attn_ln1_b': (0.0, 0.8),
     'L0_attn_ln2_g': (1.0, 0.6),
     'L0_attn_ln2_b': (0.0, 0.8)}
    factors = {'L0_attn_time_decay': 8.0,
     'L0_attn_time_first': 8.0,
     'L0_attn_tm_k': 8.0,
     'L0_attn_tm_v': 8.0,
     'L0_attn_tm_r': 8.0,
     'L0_attn_Wk': 8.0,
     'L0_attn_Wv': 8.0,
     'L0_attn_Wr': 8.0,
     'L0_attn_Wo': 8.0,
     'L0_attn_cm_k': 8.0,
     'L0_attn_cm_r': 8.0,
     'L0_attn_Wck': 8.0,
     'L0_attn_Wcr': 8.0,
     'L0_attn_Wcv': 8.0}
    for name, (base, spread) in spreads.items():
        noise = np.random.default_rng([zlib.crc32(name.encode()), seed]).standard_normal(out[name].shape)
        drawn = base * np.exp(spread * noise) if base else spread * noise
        out[name] = jnp.asarray(drawn.astype(out[name].dtype))
    for name, factor in factors.items():
        out[name] = (out[name] * factor).astype(out[name].dtype)
    return out
```

```python
from contextlib import ExitStack

import concourse.bass as bass
from concourse import mybir

ALU = mybir.AluOpType
ACT = mybir.ActivationFunctionType
F32 = mybir.dt.float32
F32R = mybir.dt.float32r

P = 128
EPS = 1e-5
NEG = -1e38
VECTORS = ["ln1_g", "ln1_b", "ln2_g", "ln2_b", "time_decay", "time_first", "tm_k", "tm_v", "tm_r", "cm_k", "cm_r"]


def build(nc, x, ffn_w, ffn_b, ids, gates, vectors, wk, wv, wr, wo, wcr, wck, wcv, out):
    B, T, C = x.shape
    HID = wck.shape[1]
    K = ids.shape[0]
    N_ADAPTERS = ffn_w.shape[0]
    CH = C // P
    NT = T // P
    HB = HID // P
    BANKS = 2
    TB = NT // BANKS
    LAG = 2
    PAD = T + 1

    with ExitStack() as ctx:
        def sb(name, shape, dt=F32):
            return ctx.enter_context(nc.sbuf_tensor(name, shape, dt))

        def sem(name):
            return ctx.enter_context(nc.semaphore(name))

        ident = sb("ident", [P, P])
        vec = sb("vec", [P, len(VECTORS), CH])
        V = {n: vec[:, i, :] for i, n in enumerate(VECTORS)}
        decay = sb("decay", [P, CH])
        nhalf = sb("nhalf", [P, NT])
        minus = sb("minus", [P, NT])
        eps = sb("eps", [P, NT])
        carried = sb("carried", [P, 32])
        gates_bc = sb("gates_bc", [P, K])
        gate_col = sb("gate_col", [K, 1])
        gate_rows = sb("gate_rows", [K, P])
        bias_sel = sb("bias_sel", [K, C])
        bias_bc = sb("bias_bc", [P, C])
        ids_row = sb("ids_row", [1, K], ids.dtype)
        ffn_t = sb("ffn_t", [P, CH, C])
        wk_sb, wv_sb, wr_sb, wo_sb, wcr_sb = (sb(n, [P, CH, C]) for n in ("wk_sb", "wv_sb", "wr_sb", "wo_sb", "wcr_sb"))
        wck_hi = sb("wck_hi", [P, CH, HID], F32R)
        wck_lo = sb("wck_lo", [P, CH, HID], F32R)
        wcv_hi = sb("wcv_hi", [P, HB, C], F32R)
        wcv_lo = sb("wcv_lo", [P, HB, C], F32R)

        x1 = [sb(f"x1_{i}", [P, NT, C]) for i in range(2)]
        xs = [sb(f"xs_{i}", [P, NT, C]) for i in range(2)]
        norm_x = sb("norm_x", [P, NT, C])
        norm_x2 = sb("norm_x2", [P, NT, C])
        norm_att = sb("norm_att", [P, NT, C])
        xa = sb("xa", [P, NT, C])
        thc = sb("thc", [P, NT, C])
        kinds = ("x", "x1", "xa", "x2")
        bn = {k: sb(f"bn_{k}", [P, NT, 6]) for k in kinds}
        mv = {k: sb(f"mv_{k}", [P, NT, 2]) for k in kinds}
        negm = {k: sb(f"negm_{k}", [P, NT]) for k in kinds}
        vare = {k: sb(f"vare_{k}", [P, NT]) for k in kinds}
        rstd = {k: sb(f"rstd_{k}", [P, NT]) for k in kinds}
        var2 = sb("var2", [P, NT])
        rstd2 = sb("rstd2", [P, NT])
        rboth = sb("rboth", [P, NT])

        ffn_in = sb("ffn_in", [P, CH, T])
        h1 = sb("h1", [P, CH, PAD])
        h2 = sb("h2", [P, CH, PAD])
        dr = sb("dr", [P, CH, T])
        dcr = sb("dcr", [P, CH, T])
        xk = sb("xk", [P, CH, T])
        xv = sb("xv", [P, CH, T])
        xck_hi = sb("xck_hi", [P, CH, T], F32R)
        xck_lo = sb("xck_lo", [P, CH, T], F32R)
        kk_relu = sb("kk_relu", [P, 2, T])
        kk_sq = sb("kk_sq", [P, 2, T])
        kk_hi = sb("kk_hi", [P, HB, T], F32R)
        kk_lo = sb("kk_lo", [P, HB, T], F32R)
        thr = sb("thr", [P, CH, T])
        rwkv = sb("rwkv", [P, CH, T])
        xck = rwkv
        work = sb("work", [P, 9 * CH * PAD])
        pp, aa, bb, z2, z, eb_v, eb_s, e_s, e_v = (
            work[:, i * CH * PAD:(i + 1) * CH * PAD].rearrange("p (h t) -> p h t", h=CH) for i in range(9))
        sel = work[:, 0:K * CH * C].rearrange("p (k h o) -> p k h o", k=K, h=CH)
        at = K * CH * C
        wck_raw = work[:, at:at + CH * HID].rearrange("p (h o) -> p h o", h=CH)
        at += CH * HID
        wcv_raw = work[:, at:at + HB * C].rearrange("p (h o) -> p h o", h=HB)
        assert at + HB * C <= 9 * CH * PAD

        k_ps = ctx.enter_context(nc.psum_tensor("k_ps", [P, CH, T], F32))
        v_ps = ctx.enter_context(nc.psum_tensor("v_ps", [P, CH, T], F32))
        ring = [ctx.enter_context(nc.psum_tensor(f"ring{i}", [P, T], F32)) for i in range(4)]

        s_const, s_vec, s_small, s_ids, s_sel, s_pads = (sem(n) for n in ("s_const", "s_vec", "s_small", "s_ids", "s_sel", "s_pads"))
        s_wload = {n: sem(f"s_load_{n}") for n in ("wk", "wv", "wr", "wo", "wcr", "wck", "wcv")}
        s_decay, s_decay_neg, s_decay_rows, s_gates = (sem(n) for n in ("s_decay", "s_decay_neg", "s_decay_rows", "s_gates"))
        s_gate_rows, s_bias_ps, s_bias, s_ffn_acc = (sem(n) for n in ("s_gate_rows", "s_bias_ps", "s_bias", "s_ffn_acc"))
        s_wo, s_wcv_half, s_wck_hi, s_wcv_hi, s_wlo = (sem(n) for n in ("s_wo", "s_wcv_half", "s_wck_hi", "s_wcv_hi", "s_wlo"))
        x_loaded, stored = sem("x_loaded"), sem("stored")
        bn_done = {k: sem(f"bn_done_{k}") for k in kinds}
        mv_done = {k: sem(f"mv_done_{k}") for k in kinds}
        rs_steps = {k: sem(f"rs_steps_{k}") for k in kinds}
        normed = {k: sem(f"normed_{k}") for k in kinds}
        xa_done, xb_done, x2b_done, xs_done = (sem(n) for n in ("xa_done", "xb_done", "x2b_done", "xs_done"))
        turned = {k: sem(f"turned_{k}") for k in kinds}
        ffn1_in, ffn2_in, h1_done, h2_done = (sem(n) for n in ("ffn1_in", "ffn2_in", "h1_done", "h2_done"))
        d1_done, d2_done = sem("d1_done"), sem("d2_done")
        xk_done, xv_done, xr_done, xck_done, xcr_done = (sem(n) for n in ("xk_done", "xv_done", "xr_done", "xck_done", "xcr_done"))
        xck_hi_done, xck_lo_done = sem("xck_hi_done"), sem("xck_lo_done")
        y1_ps, y2_ps, o_ps, r_ps, kp_ps, vp_ps, cr_ps, kk_ps, kv_ps = (
            sem(n) for n in ("y1_ps", "y2_ps", "o_ps", "r_ps", "kp_ps", "vp_ps", "cr_ps", "kk_ps", "kv_ps"))
        x1_done, xa2_done, kvs_done, x2_done, x3_done = (sem(n) for n in ("x1_done", "xa2_done", "kvs_done", "x2_done", "x3_done"))
        thr_done, thc_done = sem("thr_done"), sem("thc_done")
        relu_done, sq_done, kkhi_done, kklo_done = (sem(n) for n in ("relu_done", "sq_done", "kkhi_done", "kklo_done"))
        pp_done, z2_done, z_done, rect2, rect, eb_done, e_done = (
            sem(n) for n in ("pp_done", "z2_done", "z_done", "rect2", "rect", "eb_done", "e_done"))
        bb_done, ev_done, aa_done, t1_done, t2_done, t3_done, den_done = (
            sem(n) for n in ("bb_done", "ev_done", "aa_done", "t1_done", "t2_done", "t3_done", "den_done"))
        ln_done, r0_done, dr0_done, rec_done, num_done, y_done, rwkv_done = (
            sem(n) for n in ("ln_done", "r0_done", "dr0_done", "rec_done", "num_done", "y_done", "rwkv_done"))

        LOW = [("turn_x", 0, ffn1_in, 2, 0), ("kk0", -2, relu_done, HB, 0), ("kk4", -2, relu_done, HB, 4), ("y1", 0, x1_done, 2, 0),
               ("o", -1, xa2_done, 2, 0), ("turn_x1", 0, h1_done, 2, 0), ("turn_xa", -1, h2_done, 2, 0), ("r", 0, thr_done, 2, 0)]
        HIGH = [("kk2", -2, relu_done, HB, 2), ("kk6", -2, relu_done, HB, 6), ("kv", -2, kvs_done, 2, 0),
                ("turn_x2", -2, ffn2_in, 2, 0), ("y2", -2, x3_done, 2, 0), ("cr", -1, thc_done, 2, 0)]

        def bank_of(stage, i):
            return ring[i if any(u[0] == stage for u in LOW) else 2 + i][:, :]

        def take_bank(pe, stage, i, j):
            order = LOW if any(u[0] == stage for u in LOW) else HIGH
            at = [u[0] for u in order].index(stage)
            step = j
            while True:
                at -= 1
                if at < 0:
                    at, step = len(order) - 1, step - 1
                    if isinstance(step, int) and step < 0:
                        return
                _, rel, reader, per, first = order[at]
                b = step + rel
                if not isinstance(b, int) or 0 <= b < B:
                    pe.wait_ge(reader, b * per + first + i + 1)
                    return

        def reused(eng, s, count, b):
            if not isinstance(b, int) or b > 0:
                eng.wait_ge(s, count)

        def has(b):
            return not isinstance(b, int) or 0 <= b < B

        carriers = []

        def own_wait(engine, b):
            if not isinstance(b, int):
                at = len(carriers)
                carriers.append(at)
                if engine is nc.vector:
                    engine.memset(carried[:, at:at + 1], 0.0)
                else:
                    engine.tensor_tensor(carried[:, at:at + 1], nhalf[:, 0:1], nhalf[:, 0:1], ALU.add)

        def tok_dram(a, b):
            return a[b, :, :].rearrange("(t p) c -> p t c", p=P)

        def tok_bank(tile, i):
            return tile[:, i * TB:(i + 1) * TB, :]

        def bank3(bank):
            return bank.rearrange("p (t c) -> p t c", t=TB)

        def steps(eng, step):
            for j in range(LAG):
                step(j, j % 2)
            with eng.Fori(LAG, B - 1, 2) as j:
                for q in range(2):
                    step(j + q, q)
            for j in range(B, B + LAG):
                step(j, j % 2)

        block = ctx.enter_context(nc.Block())

        @block.sync
        def _(sp):
            sp.sem_inc(stored, 16)
            sp.dma_start(ids_row[:, :], ids.rearrange("(a k) -> a k", a=1)).then_inc(s_ids, 16)
            sp.dma_start(x1[0][:, :, :], tok_dram(x, 0)).then_inc(x_loaded, 16)
            sp.wait_ge(s_ids, 16)
            for k in range(K):
                v = sp.value_load(ids_row[0:1, k:k + 1], min_val=0, max_val=N_ADAPTERS - 1)
                sp.dma_start(sel[:, k, :, :], ffn_w[v, :, :].rearrange("(h p) o -> p h o", p=P)).then_inc(s_sel, 16)
                sp.dma_start(bias_sel[k:k + 1, :], ffn_b[v, :].rearrange("(a c) -> a c", a=1)).then_inc(s_small, 16)

            def step(j, q):
                b = j - 2
                if has(j) and not (isinstance(j, int) and j == 0):
                    if has(b):
                        sp.wait_ge(xs_done, j - 1)
                    sp.wait_ge(x_loaded, 16 * (j - 1) + 16)
                    sp.dma_start(x1[q][:, :, :], tok_dram(x, j)).then_inc(x_loaded, 16)
                if has(b):
                    sp.wait_ge(stored, 16 * b + 16)
                    sp.wait_ge(x3_done, 2 * b + 2)
                    sp.dma_start(tok_dram(out, b), xs[q][:, :, :]).then_inc(stored, 16)

            steps(sp, step)
            sp.wait_ge(stored, 16 * (B + 1))

        @block.tensor
        def _(pe):
            def product32(bank, stationary, moving, first, last):
                return nc.tensor.matmul(bank, stationary, moving, start=first, stop=last)

            def product_split(bank, stationary, moving, first, last):
                (sh, sl), (mh, ml) = stationary, moving
                nc.tensor.matmul(bank, sh, mh, start=first, stop=False)
                nc.tensor.matmul(bank, sh, ml, start=False, stop=False)
                return nc.tensor.matmul(bank, sl, mh, start=False, stop=last)

            def turn(stage, kind, tile, b, j):
                for h in range(CH):
                    take_bank(pe, stage, h, j)
                    if h == 0:
                        pe.wait_ge(normed[kind], b + 1)
                    for t in range(NT):
                        last = nc.tensor.transpose(bank_of(stage, h)[:, t * P:(t + 1) * P], tile[:, t, h * P:(h + 1) * P], ident[:, :])
                    last.then_inc(turned[kind], 1)

            def to_tokens(stage, src, w, done, j):
                for i in range(BANKS):
                    take_bank(pe, stage, i, j)
                    for t in range(TB):
                        tok = (i * TB + t) * P
                        for h in range(CH):
                            last = product32(bank_of(stage, i)[:, t * C:(t + 1) * C], src[:, h, tok:tok + P], w[:, h, :],
                                             h == 0, h == CH - 1)
                    last.then_inc(done, 1)

            def to_channels(bank, src, w, o):
                for h in range(CH):
                    last = product32(bank, w[:, h, o * P:(o + 1) * P], src[:, h, :], h == 0, h == CH - 1)
                return last

            pe.wait_ge(s_gate_rows, 1)
            pe.wait_ge(s_small, 16 * (K + 1))
            nc.tensor.matmul(k_ps[:, 0, 0:C], gate_rows[:, :], bias_sel[:, :], start=True, stop=True).then_inc(s_bias_ps, 1)
            pe.wait_ge(s_const, 3)

            def front_rk(f, j):
                if isinstance(f, int) and f == 0:
                    for n in ("wk", "wv", "wr"):
                        pe.wait_ge(s_wload[n], 16)
                    pe.wait_ge(s_bias, 1)
                pe.wait_ge(xr_done, 2 * f + 2)
                for o in range(CH):
                    take_bank(pe, "r", o, j)
                    to_channels(bank_of("r", o), dr, wr_sb, o).then_inc(r_ps, 1)
                pe.wait_ge(xk_done, 2 * f + 2)
                for o in range(CH):
                    reused(pe, z_done, 2 * (f - 1) + o + 1, f)
                    to_channels(k_ps[:, o, :], xk, wk_sb, o).then_inc(kp_ps, 1)

            def front_v(f):
                pe.wait_ge(xv_done, 2 * f + 2)
                for o in range(CH):
                    reused(pe, t1_done, 2 * (f - 1) + o + 1, f)
                    to_channels(v_ps[:, o, :], xv, wv_sb, o).then_inc(vp_ps, 1)

            def channel_keys(e, j):
                if isinstance(e, int) and e == 0 or not isinstance(e, int):
                    pe.wait_ge(s_wck_hi, 1)
                    pe.wait_ge(s_wlo, 1)
                pe.wait_ge(xck_hi_done, 2 * e + 2)
                pe.wait_ge(xck_lo_done, 2 * e + 2)
                for n in range(HB):
                    stage, i = f"kk{n // 2 * 2}", n % 2
                    take_bank(pe, stage, i, j)
                    for h in range(CH):
                        last = product_split(bank_of(stage, i), (wck_hi[:, h, n * P:(n + 1) * P], wck_lo[:, h, n * P:(n + 1) * P]),
                                             (xck_hi[:, h, :], xck_lo[:, h, :]), h == 0, h == CH - 1)
                    last.then_inc(kk_ps, 1)

            def channel_values(e, i, j):
                if i == 0:
                    pe.wait_ge(s_wcv_hi, 1)
                    pe.wait_ge(s_wlo, 2)
                take_bank(pe, "kv", i, j)
                for t in range(TB):
                    tok = (i * TB + t) * P
                    for n in range(HB):
                        if i == 0 and t == 0:
                            pe.wait_ge(kkhi_done, HB * e + n + 1)
                            pe.wait_ge(kklo_done, HB * e + n + 1)
                        last = product_split(bank_of("kv", i)[:, t * C:(t + 1) * C],
                                             (kk_hi[:, n, tok:tok + P], kk_lo[:, n, tok:tok + P]),
                                             (wcv_hi[:, n, :], wcv_lo[:, n, :]), n == 0, n == HB - 1)
                last.then_inc(kv_ps, 1)

            def step(j, q):
                f, m, e = j, j - 1, j - 2
                if has(f):
                    turn("turn_x", "x", norm_x, f, j)
                if has(e):
                    channel_keys(e, j)
                if has(f):
                    if isinstance(f, int) and f == 0:
                        pe.wait_ge(s_ffn_acc, K)
                    pe.wait_ge(ffn1_in, 2 * f + 2)
                    to_tokens("y1", ffn_in, ffn_t, y1_ps, j)
                if has(e):
                    channel_values(e, 0, j)
                if has(m):
                    if isinstance(m, int) and m == 0:
                        pe.wait_ge(s_wo, 1)
                    pe.wait_ge(rwkv_done, 2 * m + 2)
                    to_tokens("o", rwkv, wo_sb, o_ps, j)
                if has(f):
                    turn("turn_x1", "x1", norm_att, f, j)
                if has(e):
                    channel_values(e, 1, j)
                if has(m):
                    turn("turn_xa", "xa", norm_att, m, j)
                if has(f):
                    front_rk(f, j)
                if has(e):
                    turn("turn_x2", "x2", norm_x2, e, j)
                if has(f):
                    front_v(f)
                if has(e):
                    pe.wait_ge(ffn2_in, 2 * e + 2)
                    to_tokens("y2", ffn_in, ffn_t, y2_ps, j)
                if has(m):
                    if isinstance(m, int) and m == 0:
                        pe.wait_ge(s_wload["wcr"], 16)
                    pe.wait_ge(xcr_done, 2 * m + 2)
                    to_tokens("cr", dcr, wcr_sb, cr_ps, j)

            steps(pe, step)

        @block.scalar
        def _(act):
            act.dma_start(gate_col[:, :], gates.rearrange("(k a) -> k a", a=1)).then_inc(s_small, 16)
            act.dma_start(gates_bc[:, :], gates.rearrange("(a k) -> a k", a=1).broadcast_to([P, K])).then_inc(s_gates, 16)
            act.dma_start(vec[:, :, :], vectors).then_inc(s_vec, 16)
            for n, dst, src in (("wr", wr_sb, wr), ("wk", wk_sb, wk), ("wv", wv_sb, wv), ("wo", wo_sb, wo), ("wcr", wcr_sb, wcr),
                                ("wck", wck_raw, wck), ("wcv", wcv_raw, wcv)):
                act.dma_start(dst[:, :, :], src.rearrange("(h p) o -> p h o", p=P)).then_inc(s_wload[n], 16)
            act.wait_ge(s_vec, 16)
            nc.scalar.activation(decay[:, :], V["time_decay"], ACT.Exp).then_inc(s_decay, 1)

            def evac(kind, dst, done, b):
                for h in range(CH):
                    act.wait_ge(turned[kind], 2 * b + h + 1)
                    nc.scalar.activation(dst[:, h, :], bank_of(f"turn_{kind}", h), ACT.Copy).then_inc(done, 1)

            def evac_affine(kind, dst, done, g, off, b):
                for h in range(CH):
                    act.wait_ge(turned[kind], 2 * b + h + 1)
                    nc.scalar.activation(dst[:, h, 1:PAD], bank_of(f"turn_{kind}", h), ACT.Identity,
                                         scale=V[g][:, h:h + 1], bias=V[off][:, h:h + 1]).then_inc(done, 1)

            def channel_key(b, n):
                stage, i = f"kk{n // 2 * 2}", n % 2
                c = HB * b + n
                act.wait_ge(kk_ps, c + 1)
                nc.scalar.activation(kk_relu[:, i, :], bank_of(stage, i), ACT.Relu).then_inc(relu_done, 1)
                if n > 1:
                    act.wait_ge(kklo_done, c - 1)
                act.wait_ge(relu_done, c + 1)
                nc.scalar.activation(kk_sq[:, i, :], kk_relu[:, i, :], ACT.Square).then_inc(sq_done, 1)
                act.wait_ge(sq_done, c + 1)
                nc.scalar.activation(kk_hi[:, n, :], kk_sq[:, i, :], ACT.Copy).then_inc(kkhi_done, 1)

            def exp_pairs(m):
                for src, ready, pos, neg, mid, done in ((z2, z2_done, eb_v, eb_s, rect2, eb_done), (z, z_done, e_s, e_v, rect, e_done)):
                    for h in range(CH):
                        act.wait_ge(ready, 2 * m + h + 1)
                        nc.scalar.activation(pos[:, h, 0:T], src[:, h, 0:T], ACT.Relu).then_inc(mid, 1)
                        nc.scalar.activation(neg[:, h, 0:T], src[:, h, 0:T], ACT.Relu, scale=-1.0).then_inc(mid, 1)
                    for h in range(CH):
                        act.wait_ge(mid, 4 * m + 2 * h + 2)
                        nc.scalar.activation(pos[:, h, 0:T], pos[:, h, 0:T], ACT.Exp, scale=-1.0)
                        nc.scalar.activation(neg[:, h, 0:T], neg[:, h, 0:T], ACT.Exp, scale=-1.0).then_inc(done, 1)

            def step(j, q):
                f, m, e = j, j - 1, j - 2
                if has(f):
                    evac("x", ffn_in, ffn1_in, f)
                if has(m):
                    act.preload_act_table_set("natural_log_exp_and_others")
                    exp_pairs(m)
                if has(e):
                    for n in range(HB):
                        channel_key(e, n)
                if has(m):
                    for h in range(CH):
                        act.wait_ge(den_done, 2 * m + h + 1)
                        nc.scalar.activation(eb_v[:, h, 0:T], e_v[:, h, 0:T], ACT.Ln).then_inc(ln_done, 1)
                    for h in range(CH):
                        act.wait_ge(ln_done, 2 * m + h + 1)
                        nc.scalar.activation(eb_v[:, h, 0:T], eb_v[:, h, 0:T], ACT.Exp, scale=-1.0).then_inc(r0_done, 1)
                if has(f):
                    evac_affine("x1", h1, h1_done, "ln1_g", "ln1_b", f)
                if has(m):
                    evac_affine("xa", h2, h2_done, "ln2_g", "ln2_b", m)
                    for h in range(CH):
                        act.wait_ge(xck_done, 2 * m + h + 1)
                        nc.scalar.activation(xck_hi[:, h, :], xck[:, h, :], ACT.Copy).then_inc(xck_hi_done, 1)
                if has(f):
                    for h in range(CH):
                        act.wait_ge(r_ps, 2 * f + h + 1)
                        nc.scalar.activation(thr[:, h, :], bank_of("r", h), ACT.Tanh, scale=0.5).then_inc(thr_done, 1)
                if has(e):
                    evac("x2", ffn_in, ffn2_in, e)
                if has(m):
                    for i in range(BANKS):
                        act.wait_ge(cr_ps, 2 * m + i + 1)
                        nc.scalar.activation(tok_bank(thc, i), bank3(bank_of("cr", i)), ACT.Tanh, scale=0.5).then_inc(thc_done, 1)

            steps(act, step)

        @block.vector
        def _(dve):
            dve.wait_ge(s_decay, 1)
            nc.vector.tensor_scalar(decay[:, :], decay[:, :], -1.0, None, ALU.mult).then_inc(s_decay_neg, 1)
            dve.wait_ge(s_small, 16 * (K + 1))
            dve.wait_ge(s_const, 2)
            nc.vector.tensor_scalar(gate_rows[:, :], gate_rows[:, :], gate_col[:, 0:1], 0.5, ALU.mult, ALU.mult).then_inc(s_gate_rows, 1)
            dve.wait_ge(s_gates, 16)
            nc.vector.tensor_scalar(gates_bc[:, :], gates_bc[:, :], 0.5, None, ALU.mult).then_inc(s_gates, 1)

            def stats(kind, tile, b):
                for t in range(NT):
                    last = nc.vector.bn_stats(bn[kind][:, t, :], tile[:, t, :])
                last.then_inc(bn_done[kind], 1)
                dve.wait_ge(bn_done[kind], b + 1)
                own_wait(nc.vector, b)
                for t in range(NT):
                    last = nc.vector.bn_aggr(mv[kind][:, t, :], bn[kind][:, t, :])
                last.then_inc(mv_done[kind], 1)

            def ffn_weights():
                dve.wait_ge(s_gates, 17)
                dve.wait_ge(s_sel, 16 * K)
                for k in range(K):
                    g = gates_bc[:, k:k + 1]
                    if k == 0:
                        nc.vector.tensor_scalar(ffn_t[:, :, :], sel[:, 0, :, :], g, None, ALU.mult).then_inc(s_ffn_acc, 1)
                    else:
                        dve.wait_ge(s_ffn_acc, k)
                        nc.vector.scalar_tensor_tensor(ffn_t[:, :, :], sel[:, k, :, :], g, ffn_t[:, :, :], ALU.mult, ALU.add).then_inc(s_ffn_acc, 1)
                dve.wait_ge(s_bias_ps, 1)
                nc.vector.tensor_copy(bias_bc[:, :], k_ps[:, 0, 0:C]).then_inc(s_bias, 1)

            def other_weights():
                dve.wait_ge(s_wload["wo"], 16)
                nc.vector.tensor_scalar(wo_sb[:, :, :], wo_sb[:, :, :], 0.5, None, ALU.mult).then_inc(s_wo, 1)
                dve.wait_ge(s_wload["wck"], 16)
                nc.vector.tensor_copy(wck_hi[:, :, :], wck_raw).then_inc(s_wck_hi, 1)
                dve.wait_ge(s_wload["wcv"], 16)
                nc.vector.tensor_scalar(wcv_raw, wcv_raw, 0.5, None, ALU.mult).then_inc(s_wcv_half, 1)
                dve.wait_ge(s_wck_hi, 1)
                nc.vector.tensor_tensor(wck_lo[:, :, :], wck_raw, wck_hi[:, :, :].bitcast(F32), ALU.subtract).then_inc(s_wlo, 1)
                dve.wait_ge(s_wcv_half, 1)
                nc.vector.tensor_copy(wcv_hi[:, :, :], wcv_raw).then_inc(s_wcv_hi, 1)
                dve.wait_ge(s_wcv_hi, 1)
                nc.vector.tensor_tensor(wcv_lo[:, :, :], wcv_raw, wcv_hi[:, :, :].bitcast(F32), ALU.subtract).then_inc(s_wlo, 1)
                dve.wait_ge(s_wlo, 2)
                nc.vector.memset(pp[:, :, 0:1], NEG)
                nc.vector.memset(aa[:, :, 0:1], 0.0)
                nc.vector.memset(bb[:, :, 0:1], 0.0).then_inc(s_pads, 1)

            def wkv_exponents(m):
                for h in range(CH):
                    dve.wait_ge(kp_ps, 2 * m + h + 1)
                    nc.vector.tensor_tensor_scan(pp[:, h, 1:PAD], decay[:, h:h + 1].to_broadcast([P, T]), k_ps[:, h, :],
                                                 NEG, ALU.add, ALU.max).then_inc(pp_done, 1)
                for h in range(CH):
                    dve.wait_ge(pp_done, 2 * m + h + 1)
                    nc.vector.scalar_tensor_tensor(z2[:, h, 0:T], pp[:, h, 0:T], decay[:, h:h + 1], k_ps[:, h, :],
                                                   ALU.add, ALU.subtract).then_inc(z2_done, 1)
                for h in range(CH):
                    nc.vector.scalar_tensor_tensor(z[:, h, 0:T], k_ps[:, h, :], V["time_first"][:, h:h + 1], pp[:, h, 0:T],
                                                   ALU.add, ALU.subtract).then_inc(z_done, 1)

            def wkv_states(m):
                for h in range(CH):
                    dve.wait_ge(eb_done, 2 * m + h + 1)
                    nc.vector.tensor_tensor_scan(bb[:, h, 1:PAD], eb_s[:, h, 0:T], eb_v[:, h, 0:T], 0.0, ALU.mult, ALU.add).then_inc(bb_done, 1)
                    dve.wait_ge(vp_ps, 2 * m + h + 1)
                    nc.vector.tensor_tensor(z2[:, h, 0:T], eb_v[:, h, 0:T], v_ps[:, h, :], ALU.mult).then_inc(ev_done, 1)
                for h in range(CH):
                    dve.wait_ge(ev_done, 2 * m + h + 1)
                    nc.vector.tensor_tensor_scan(aa[:, h, 1:PAD], eb_s[:, h, 0:T], z2[:, h, 0:T], 0.0, ALU.mult, ALU.add).then_inc(aa_done, 1)
                for h in range(CH):
                    dve.wait_ge(e_done, 2 * m + h + 1)
                    nc.vector.tensor_tensor(z[:, h, 0:T], e_v[:, h, 0:T], v_ps[:, h, :], ALU.mult).then_inc(t1_done, 1)
                for h in range(CH):
                    dve.wait_ge(t3_done, 2 * m + h + 1)
                    nc.vector.tensor_tensor(e_v[:, h, 0:T], e_v[:, h, 0:T], eb_v[:, h, 0:T], ALU.add).then_inc(den_done, 1)

            def wkv_quotient(m):
                for h in range(CH):
                    dve.wait_ge(t2_done, 2 * m + h + 1)
                    dve.wait_ge(t1_done, 2 * m + h + 1)
                    nc.vector.tensor_tensor(z[:, h, 0:T], z[:, h, 0:T], z2[:, h, 0:T], ALU.add).then_inc(num_done, 1)
                for h in range(CH):
                    dve.wait_ge(dr0_done, 2 * m + h + 1)
                    nc.vector.scalar_tensor_tensor(eb_s[:, h, 0:T], eb_s[:, h, 0:T], 2.0, eb_v[:, h, 0:T], ALU.subtract, ALU.mult,
                                                   reverse0=True).then_inc(rec_done, 1)
                for h in range(CH):
                    dve.wait_ge(rec_done, 2 * m + h + 1)
                    dve.wait_ge(num_done, 2 * m + h + 1)
                    nc.vector.tensor_tensor(z[:, h, 0:T], z[:, h, 0:T], eb_s[:, h, 0:T], ALU.mult).then_inc(y_done, 1)
                for h in range(CH):
                    dve.wait_ge(y_done, 2 * m + h + 1)
                    dve.wait_ge(thr_done, 2 * m + h + 1)
                    nc.vector.scalar_tensor_tensor(rwkv[:, h, :], thr[:, h, :], 1.0, z[:, h, 0:T], ALU.add, ALU.mult).then_inc(rwkv_done, 1)

            def key_rests(e, blocks):
                for n in blocks:
                    dve.wait_ge(kkhi_done, HB * e + n + 1)
                    nc.vector.tensor_tensor(kk_lo[:, n, :], kk_sq[:, n % 2, :], kk_hi[:, n, :].bitcast(F32), ALU.subtract).then_inc(kklo_done, 1)

            def value_sum(e, i, q):
                dve.wait_ge(kv_ps, 2 * e + i + 1)
                dve.wait_ge(thc_done, 2 * e + i + 1)
                nc.vector.scalar_tensor_tensor(tok_bank(thc, i), tok_bank(thc, i), 1.0, bank3(bank_of("kv", i)), ALU.add, ALU.mult).then_inc(kvs_done, 1)
                dve.wait_ge(kvs_done, 2 * e + i + 1)
                dve.wait_ge(xs_done, e + 1)
                nc.vector.tensor_tensor(tok_bank(xs[q], i), tok_bank(xs[q], i), tok_bank(thc, i), ALU.add).then_inc(x2_done, 1)

            def mix(dst, d, h, prev, m, done):
                for c in range(CH):
                    nc.vector.scalar_tensor_tensor(dst[:, c, :], d[:, c, :], V[m][:, c:c + 1], h[:, c, prev:prev + T],
                                                   ALU.mult, ALU.add).then_inc(done, 1)

            def step(j, q):
                f, m, e = j, j - 1, j - 2
                if has(f):
                    dve.wait_ge(x_loaded, 16 * f + 16)
                    stats("x", x1[q], f)
                if isinstance(j, int) and j == 0:
                    ffn_weights()
                if isinstance(j, int) and j == 1:
                    dve.wait_ge(s_pads, 1)
                if has(m):
                    wkv_exponents(m)
                if has(e):
                    key_rests(e, range(HB))
                if has(m):
                    wkv_states(m)
                    wkv_quotient(m)
                if has(f):
                    for i in range(BANKS):
                        dve.wait_ge(y1_ps, 2 * f + i + 1)
                        dve.wait_ge(xb_done, f + 1)
                        nc.vector.tensor_tensor(tok_bank(x1[q], i), tok_bank(x1[q], i), bank3(bank_of("y1", i)), ALU.add).then_inc(x1_done, 1)
                    dve.wait_ge(x1_done, 2 * f + 2)
                    stats("x1", x1[q], f)
                if has(e):
                    value_sum(e, 0, q)
                if has(m):
                    for i in range(BANKS):
                        dve.wait_ge(o_ps, 2 * m + i + 1)
                        dve.wait_ge(xa_done, m + 1)
                        nc.vector.tensor_tensor(tok_bank(xa, i), tok_bank(xa, i), bank3(bank_of("o", i)), ALU.add).then_inc(xa2_done, 1)
                    dve.wait_ge(xa2_done, 2 * m + 2)
                    stats("xa", xa, m)
                if has(e):
                    value_sum(e, 1, q)
                    dve.wait_ge(x2_done, 2 * e + 2)
                    stats("x2", xs[q], e)
                if isinstance(j, int) and j == 0:
                    other_weights()
                if has(f):
                    dve.wait_ge(d1_done, f + 1)
                    mix(xk, dr, h1, 0, "tm_k", xk_done)
                    mix(xv, dr, h1, 0, "tm_v", xv_done)
                    mix(dr, dr, h1, 0, "tm_r", xr_done)
                if has(m):
                    dve.wait_ge(d2_done, m + 1)
                    mix(xck, dcr, h2, 0, "cm_k", xck_done)
                    mix(dcr, dcr, h2, 0, "cm_r", xcr_done)
                if has(e):
                    for i in range(BANKS):
                        dve.wait_ge(y2_ps, 2 * e + i + 1)
                        dve.wait_ge(x2b_done, e + 1)
                        nc.vector.tensor_tensor(tok_bank(xs[q], i), tok_bank(xs[q], i), bank3(bank_of("y2", i)), ALU.add).then_inc(x3_done, 1)

            steps(dve, step)

        @block.gpsimd
        def _(pool):
            nc.gpsimd.memset(ident[:, :], 0.0).then_inc(s_const, 1)
            nc.gpsimd.memset(gate_rows[:, :], 1.0).then_inc(s_const, 1)
            pool.wait_ge(s_const, 1)
            nc.gpsimd.affine_select(out=ident[:, :], in_=ident[:, :], compare_op=ALU.not_equal, fill=1.0, base=0,
                                    pattern=[[-1, P]], channel_multiplier=1).then_inc(s_const, 1)
            nc.gpsimd.memset(nhalf[:, :], -0.5)
            nc.gpsimd.memset(minus[:, :], -1.0)
            nc.gpsimd.memset(eps[:, :], EPS)
            nc.gpsimd.memset(h1[:, :, 0:1], 0.0)
            nc.gpsimd.memset(h2[:, :, 0:1], 0.0).then_inc(s_const, 1)
            pool.wait_ge(s_const, 4)

            def inverse_std(kind, b, per):
                c = per * b
                pool.wait_ge(mv_done[kind], b + 1)
                nc.gpsimd.tensor_tensor(vare[kind][:, :], mv[kind][:, :, 1], eps[:, :], ALU.add).then_inc(rs_steps[kind], 1)
                nc.gpsimd.tensor_tensor(negm[kind][:, :], mv[kind][:, :, 0], minus[:, :], ALU.mult).then_inc(rs_steps[kind], 1)
                pool.wait_ge(rs_steps[kind], c + 2)
                nc.gpsimd.tensor_tensor(rstd[kind][:, :], vare[kind][:, :], nhalf[:, :], ALU.pow).then_inc(rs_steps[kind], 1)
                pool.wait_ge(rs_steps[kind], c + 3)
                own_wait(nc.gpsimd, b)

            def centre_scale(dst, src, kind, scale, done):
                for t in range(NT):
                    last = nc.gpsimd.tensor_scalar(dst[:, t, :], src[:, t, :], negm[kind][:, t:t + 1], scale[:, t:t + 1], ALU.add, ALU.mult)
                last.then_inc(done, 1)

            def double_inverse_std(f):
                k, c = "x1", 8 * f
                inverse_std(k, f, 8)
                nc.gpsimd.tensor_tensor(var2[:, :], rstd[k][:, :], rstd[k][:, :], ALU.mult).then_inc(rs_steps[k], 1)
                pool.wait_ge(rs_steps[k], c + 4)
                nc.gpsimd.tensor_tensor(var2[:, :], var2[:, :], mv[k][:, :, 1], ALU.mult).then_inc(rs_steps[k], 1)
                pool.wait_ge(rs_steps[k], c + 5)
                nc.gpsimd.tensor_tensor(var2[:, :], var2[:, :], eps[:, :], ALU.add).then_inc(rs_steps[k], 1)
                pool.wait_ge(rs_steps[k], c + 6)
                nc.gpsimd.tensor_tensor(rstd2[:, :], var2[:, :], nhalf[:, :], ALU.pow).then_inc(rs_steps[k], 1)
                pool.wait_ge(rs_steps[k], c + 7)
                nc.gpsimd.tensor_tensor(rboth[:, :], rstd2[:, :], rstd[k][:, :], ALU.mult).then_inc(rs_steps[k], 1)
                pool.wait_ge(rs_steps[k], c + 8)
                own_wait(nc.gpsimd, f)

            def add_bias(tile, done):
                last = nc.gpsimd.tensor_tensor(tile, tile, bias_bc[:, :].rearrange("p (a c) -> p a c", a=1).broadcast_to([P, NT, C]), ALU.add)
                last.then_inc(done, 1)

            def step(j, q):
                f, m, e = j, j - 1, j - 2
                if has(f):
                    inverse_std("x", f, 3)
                    centre_scale(norm_x, x1[q], "x", rstd["x"], normed["x"])
                    if isinstance(f, int) and f == 0:
                        pool.wait_ge(s_bias, 1)
                    pool.wait_ge(normed["x"], f + 1)
                    add_bias(x1[q][:, :, :], xb_done)
                if has(m):
                    for h in range(CH):
                        pool.wait_ge(bb_done, 2 * m + h + 1)
                        pool.wait_ge(e_done, 2 * m + h + 1)
                        pool.wait_ge(ev_done, 2 * m + h + 1)
                        nc.gpsimd.tensor_tensor(eb_v[:, h, 0:T], e_s[:, h, 0:T], bb[:, h, 0:T], ALU.mult).then_inc(t3_done, 1)
                    for h in range(CH):
                        pool.wait_ge(aa_done, 2 * m + h + 1)
                        nc.gpsimd.tensor_tensor(z2[:, h, 0:T], e_s[:, h, 0:T], aa[:, h, 0:T], ALU.mult).then_inc(t2_done, 1)
                    for h in range(CH):
                        pool.wait_ge(r0_done, 2 * m + h + 1)
                        nc.gpsimd.tensor_tensor(eb_s[:, h, 0:T], e_v[:, h, 0:T], eb_v[:, h, 0:T], ALU.mult).then_inc(dr0_done, 1)
                if has(f):
                    double_inverse_std(f)
                    centre_scale(norm_att, x1[q], "x1", rboth, normed["x1"])
                if has(m):
                    inverse_std("xa", m, 3)
                    if has(f):
                        pool.wait_ge(turned["x1"], 2 * f + 2)
                        own_wait(nc.gpsimd, f)
                    centre_scale(norm_att, xa, "xa", rstd["xa"], normed["xa"])
                if has(f):
                    pool.wait_ge(h1_done, 2 * f + 2)
                    nc.gpsimd.tensor_tensor(dr[:, :, :], h1[:, :, 1:PAD], h1[:, :, 0:T], ALU.subtract).then_inc(d1_done, 1)
                if has(m):
                    if isinstance(m, int) and m < 2:
                        pass
                    else:
                        pool.wait_ge(stored, 16 * (m - 1) + 16)
                    nc.gpsimd.tensor_tensor(xs[1 - q][:, :, :], x1[1 - q][:, :, :], xa[:, :, :], ALU.add).then_inc(xs_done, 1)
                if has(e):
                    inverse_std("x2", e, 3)
                    centre_scale(norm_x2, xs[q], "x2", rstd["x2"], normed["x2"])
                if has(m):
                    pool.wait_ge(h2_done, 2 * m + 2)
                    nc.gpsimd.tensor_tensor(dcr[:, :, :], h2[:, :, 1:PAD], h2[:, :, 0:T], ALU.subtract).then_inc(d2_done, 1)
                    pool.wait_ge(xck_hi_done, 2 * m + 2)
                    nc.gpsimd.tensor_tensor(xck_lo[:, :, :], xck[:, :, :], xck_hi[:, :, :].bitcast(F32), ALU.subtract).then_inc(xck_lo_done, 2)
                if has(e):
                    pool.wait_ge(normed["x2"], e + 1)
                    add_bias(xs[q][:, :, :], x2b_done)
                if has(f):
                    centre_scale(xa, x1[q], "x1", rstd["x1"], xa_done)

            steps(pool, step)


_INS = ["x", "ffn_w", "ffn_b", "ids", "gates", "vectors", "wk", "wv", "wr", "wo", "wcr", "wck", "wcv"]


def kernel(**inputs):
    import numpy as _np
    import concourse.bacc as _bacc
    from concourse import mybir as _mybir
    from concourse.bass_utils import run_bass_kernel_spmd as _run

    def given(name):
        return _np.asarray(inputs[name])

    def turned(name):
        return given(name).T

    laid = {
        "x": given("L0_attn_x"),
        "ffn_w": given("L0_ffn_W").transpose(0, 2, 1),
        "ffn_b": given("L0_ffn_b"),
        "ids": given("L0_ffn_ids"),
        "gates": given("L0_ffn_weights"),
        "vectors": _np.stack([given(f"L0_attn_{n}").reshape(-1, P) for n in VECTORS]).transpose(2, 0, 1),
        "wk": turned("L0_attn_Wk"), "wv": turned("L0_attn_Wv"), "wr": turned("L0_attn_Wr"), "wo": turned("L0_attn_Wo"),
        "wcr": turned("L0_attn_Wcr"), "wck": turned("L0_attn_Wck"), "wcv": turned("L0_attn_Wcv"),
    }
    nc = _bacc.Bacc("TRN2", target_bir_lowering=False, num_devices=1)
    arrays, args = {}, []
    for name in _INS:
        a = _np.ascontiguousarray(laid[name])
        arrays[f"in_{name}_dram"] = a
        args.append(nc.dram_tensor(f"in_{name}_dram", a.shape, _mybir.dt.from_np(a.dtype), kind="ExternalInput").ap())
    shape = laid["x"].shape
    args.append(nc.dram_tensor("out_0_dram", shape, _mybir.dt.from_np(_np.dtype("float32")), kind="ExternalOutput").ap())
    build(nc, *args)
    r = _run(nc, [arrays], core_ids=[0])
    return r.results[0]["out_0_dram"]
```

```python
from contextlib import ExitStack

import concourse.bass as bass
from concourse import mybir

ALU = mybir.AluOpType
ACT = mybir.ActivationFunctionType
F32 = mybir.dt.float32
F32R = mybir.dt.float32r

P = 128
EPS = 1e-5
NEG = -1e38
VECTORS = ["ln1_g", "ln1_b", "ln2_g", "ln2_b", "time_decay", "time_first", "tm_k", "tm_v", "tm_r", "cm_k", "cm_r"]


def build(nc, x, ffn_w, ffn_b, ids, gates, vectors, wk, wv, wr, wo, wcr, wck, wcv, out):
    B, T, C = x.shape
    HID = wck.shape[1]
    K = ids.shape[0]
    N_ADAPTERS = ffn_w.shape[0]
    CH = C // P
    NT = T // P
    HB = HID // P
    BANKS = 2
    TB = NT // BANKS
    KK_BUFS = 4
    ACT_HIGHS = (0, 2, 4)
    POOL_RESTS = (1, 3, 5)
    LAG = 2
    PAD = T + 1

    with ExitStack() as ctx:
        def sb(name, shape, dt=F32):
            return ctx.enter_context(nc.sbuf_tensor(name, shape, dt))

        def sem(name):
            return ctx.enter_context(nc.semaphore(name))

        ident = sb("ident", [P, P])
        vec = sb("vec", [P, len(VECTORS), CH])
        V = {n: vec[:, i, :] for i, n in enumerate(VECTORS)}
        decay = sb("decay", [P, CH])
        nhalf = sb("nhalf", [P, NT])
        minus = sb("minus", [P, NT])
        eps = sb("eps", [P, NT])
        eps_sq = sb("eps_sq", [P, NT])
        one_eps = sb("one_eps", [P, NT])
        carried = sb("carried", [P, 32])
        gates_bc = sb("gates_bc", [P, K])
        gate_col = sb("gate_col", [K, 1])
        gate_rows = sb("gate_rows", [K, P])
        bias_sel = sb("bias_sel", [K, C])
        bias_bc = sb("bias_bc", [P, C])
        ids_row = sb("ids_row", [1, K], ids.dtype)
        ffn_t = sb("ffn_t", [P, CH, C])
        wk_sb, wv_sb, wr_sb, wo_sb, wcr_sb = (sb(n, [P, CH, C]) for n in ("wk_sb", "wv_sb", "wr_sb", "wo_sb", "wcr_sb"))
        wck_hi = sb("wck_hi", [P, CH, HID], F32R)
        wck_lo = sb("wck_lo", [P, CH, HID], F32R)
        wcv_hi = sb("wcv_hi", [P, HB, C], F32R)
        wcv_lo = sb("wcv_lo", [P, HB, C], F32R)

        x1 = [sb(f"x1_{i}", [P, NT, C]) for i in range(2)]
        xs = [sb(f"xs_{i}", [P, NT, C]) for i in range(2)]
        norm_x = sb("norm_x", [P, NT, C])
        norm_x2 = sb("norm_x2", [P, NT, C])
        norm_att = sb("norm_att", [P, NT, C])
        xa = sb("xa", [P, NT, C])
        thc = sb("thc", [P, NT, C])
        kinds = ("x", "x1", "xa", "x2")
        bn = {k: sb(f"bn_{k}", [P, NT, 6]) for k in kinds}
        mv = {k: sb(f"mv_{k}", [P, NT, 2]) for k in kinds}
        negm = {k: sb(f"negm_{k}", [P, NT]) for k in kinds}
        vare = {k: sb(f"vare_{k}", [P, NT]) for k in kinds}
        rstd = {k: sb(f"rstd_{k}", [P, NT]) for k in kinds}
        both = sb("both", [P, NT])
        rboth = sb("rboth", [P, NT])

        ffn_in = sb("ffn_in", [P, CH, T])
        h1 = sb("h1", [P, CH, PAD])
        h2 = sb("h2", [P, CH, PAD])
        dr = sb("dr", [P, CH, T])
        dcr = sb("dcr", [P, CH, T])
        xk = sb("xk", [P, CH, T])
        xv = sb("xv", [P, CH, T])
        xck_hi = sb("xck_hi", [P, CH, T], F32R)
        xck_lo = sb("xck_lo", [P, CH, T], F32R)
        kk = sb("kk", [P, KK_BUFS, T])
        kk_hi = sb("kk_hi", [P, HB, T], F32R)
        kk_lo = sb("kk_lo", [P, HB, T], F32R)
        thr = sb("thr", [P, CH, T])
        rwkv = sb("rwkv", [P, CH, T])
        xck = rwkv
        work = sb("work", [P, 9 * CH * PAD])
        pp, aa, bb, z2, z, eb_v, eb_s, e_s, e_v = (
            work[:, i * CH * PAD:(i + 1) * CH * PAD].rearrange("p (h t) -> p h t", h=CH) for i in range(9))
        sel = work[:, 0:K * CH * C].rearrange("p (k h o) -> p k h o", k=K, h=CH)
        at = K * CH * C
        wck_raw = work[:, at:at + CH * HID].rearrange("p (h o) -> p h o", h=CH)
        at += CH * HID
        wcv_raw = work[:, at:at + HB * C].rearrange("p (h o) -> p h o", h=HB)
        assert at + HB * C <= 9 * CH * PAD

        k_ps = ctx.enter_context(nc.psum_tensor("k_ps", [P, CH, T], F32))
        v_ps = ctx.enter_context(nc.psum_tensor("v_ps", [P, CH, T], F32))
        ring = [ctx.enter_context(nc.psum_tensor(f"ring{i}", [P, T], F32)) for i in range(4)]

        s_const, s_vec, s_small, s_ids, s_sel, s_pads = (sem(n) for n in ("s_const", "s_vec", "s_small", "s_ids", "s_sel", "s_pads"))
        s_wload = {n: sem(f"s_load_{n}") for n in ("wk", "wv", "wr", "wo", "wcr", "wck", "wcv")}
        s_decay, s_decay_neg, s_decay_rows, s_gates = (sem(n) for n in ("s_decay", "s_decay_neg", "s_decay_rows", "s_gates"))
        s_gate_rows, s_bias_ps, s_bias, s_ffn_acc = (sem(n) for n in ("s_gate_rows", "s_bias_ps", "s_bias", "s_ffn_acc"))
        s_wo, s_wcv_half, s_wck_hi, s_wcv_hi, s_wlo = (sem(n) for n in ("s_wo", "s_wcv_half", "s_wck_hi", "s_wcv_hi", "s_wlo"))
        x_loaded, stored = sem("x_loaded"), sem("stored")
        bn_done = {k: sem(f"bn_done_{k}") for k in kinds}
        mv_done = {k: sem(f"mv_done_{k}") for k in kinds}
        rs_steps = {k: sem(f"rs_steps_{k}") for k in kinds}
        normed = {k: sem(f"normed_{k}") for k in kinds}
        rs1_steps = sem("rs1_steps")
        xa_done, xb_done, x2b_done, xs_done = (sem(n) for n in ("xa_done", "xb_done", "x2b_done", "xs_done"))
        turned = {k: sem(f"turned_{k}") for k in kinds}
        ffn1_in, ffn2_in, h1_done, h2_done = (sem(n) for n in ("ffn1_in", "ffn2_in", "h1_done", "h2_done"))
        d1_done, d2_done = sem("d1_done"), sem("d2_done")
        xk_done, xv_done, xr_done, xck_done, xcr_done = (sem(n) for n in ("xk_done", "xv_done", "xr_done", "xck_done", "xcr_done"))
        xck_hi_done, xck_lo_done = sem("xck_hi_done"), sem("xck_lo_done")
        y1_ps, y2_ps, o_ps, r_ps, kp_ps, vp_ps, cr_ps, kk_ps, kv_ps = (
            sem(n) for n in ("y1_ps", "y2_ps", "o_ps", "r_ps", "kp_ps", "vp_ps", "cr_ps", "kk_ps", "kv_ps"))
        x1_done, xa2_done, kvs_done, x2_done, x3_done = (sem(n) for n in ("x1_done", "xa2_done", "kvs_done", "x2_done", "x3_done"))
        thr_done, thc_done = sem("thr_done"), sem("thc_done")
        relu_done, sq_done = sem("relu_done"), sem("sq_done")
        high_act, high_dve = sem("high_act"), sem("high_dve")
        rest_pool, rest_dve = sem("rest_pool"), sem("rest_dve")
        pp_done, z2_done, z_done, rect2, rect, eb_done, e_done = (
            sem(n) for n in ("pp_done", "z2_done", "z_done", "rect2", "rect", "eb_done", "e_done"))
        bb_done, ev_done, aa_done, t1_done, t2_done, t3_done, den_done = (
            sem(n) for n in ("bb_done", "ev_done", "aa_done", "t1_done", "t2_done", "t3_done", "den_done"))
        ln_done, r0_done, dr0_done, rec_done, num_done, y_done, rwkv_done = (
            sem(n) for n in ("ln_done", "r0_done", "dr0_done", "rec_done", "num_done", "y_done", "rwkv_done"))

        SEED = 2

        def pair(s, seed=0):
            return lambda b, i: (s, seed + 2 * b + i + 1)

        def keys_read(n):
            return lambda b, i: (relu_done, HB * b + n + i + 1)

        LOW = [("kk0", -2, keys_read(0)), ("kk4", -2, keys_read(4)), ("turn_x", 0, pair(ffn1_in)), ("y1", 0, pair(x1_done)),
               ("o", -1, pair(xa2_done)), ("cr", -2, pair(thc_done)), ("turn_x1", 0, pair(h1_done)), ("turn_xa", -1, pair(h2_done)),
               ("r", 0, pair(thr_done))]
        HIGH = [("kk2", -2, keys_read(2)), ("kk6", -2, keys_read(6)), ("kv", -2, pair(kvs_done)), ("turn_x2", -2, pair(ffn2_in)),
                ("y2", -2, pair(x3_done, SEED))]

        def bank_of(stage, i):
            return ring[i if any(u[0] == stage for u in LOW) else 2 + i][:, :]

        def take_bank(pe, stage, i, j):
            order = LOW if any(u[0] == stage for u in LOW) else HIGH
            at = [u[0] for u in order].index(stage)
            step = j
            while True:
                at -= 1
                if at < 0:
                    at, step = len(order) - 1, step - 1
                    if isinstance(step, int) and step < 0:
                        return
                _, rel, last_read = order[at]
                b = step + rel
                if not isinstance(b, int) or 0 <= b < B:
                    pe.wait_ge(*last_read(b, i))
                    return

        def reused(eng, s, count, b):
            if not isinstance(b, int) or b > 0:
                eng.wait_ge(s, count)

        def has(b):
            return not isinstance(b, int) or 0 <= b < B

        def high_done(b, n):
            mine = [i for i in range(HB) if (i in ACT_HIGHS) == (n in ACT_HIGHS)]
            return (high_act if n in ACT_HIGHS else high_dve), len(mine) * b + mine.index(n) + 1

        def rest_done(b, n):
            mine = [i for i in range(HB) if (i in POOL_RESTS) == (n in POOL_RESTS)]
            return (rest_pool if n in POOL_RESTS else rest_dve), len(mine) * b + mine.index(n) + 1

        def key_rest(engine, eng, b, n):
            eng.wait_ge(*high_done(b, n))
            engine.tensor_tensor(kk_lo[:, n, :], kk[:, n % KK_BUFS, :], kk_hi[:, n, :].bitcast(F32), ALU.subtract).then_inc(rest_done(b, n)[0], 1)

        carriers = []

        def own_wait(engine, b):
            if not isinstance(b, int):
                at = len(carriers)
                carriers.append(at)
                if engine is nc.vector:
                    engine.memset(carried[:, at:at + 1], 0.0)
                else:
                    engine.tensor_tensor(carried[:, at:at + 1], nhalf[:, 0:1], nhalf[:, 0:1], ALU.add)

        def tok_dram(a, b):
            return a[b, :, :].rearrange("(t p) c -> p t c", p=P)

        def tok_bank(tile, i):
            return tile[:, i * TB:(i + 1) * TB, :]

        def bank3(bank):
            return bank.rearrange("p (t c) -> p t c", t=TB)

        def steps(eng, step):
            for j in range(LAG):
                step(j, j % 2)
            with eng.Fori(LAG, B - 1, 2) as j:
                for q in range(2):
                    step(j + q, q)
            for j in range(B, B + LAG):
                step(j, j % 2)

        block = ctx.enter_context(nc.Block())

        @block.sync
        def _(sp):
            sp.sem_inc(stored, 16)
            sp.dma_start(ids_row[:, :], ids.rearrange("(a k) -> a k", a=1)).then_inc(s_ids, 16)
            sp.dma_start(x1[0][:, :, :], tok_dram(x, 0)).then_inc(x_loaded, 16)
            sp.wait_ge(s_ids, 16)
            for k in range(K):
                v = sp.value_load(ids_row[0:1, k:k + 1], min_val=0, max_val=N_ADAPTERS - 1)
                sp.dma_start(sel[:, k, :, :], ffn_w[v, :, :].rearrange("(h p) o -> p h o", p=P)).then_inc(s_sel, 16)
                sp.dma_start(bias_sel[k:k + 1, :], ffn_b[v, :].rearrange("(a c) -> a c", a=1)).then_inc(s_small, 16)

            def load(j, q):
                if isinstance(j, int) and (j == 0 or j >= B):
                    return
                if has(j - 2):
                    sp.wait_ge(xs_done, j - 1)
                sp.wait_ge(x_loaded, 16 * (j - 1) + 16)
                sp.dma_start(x1[q][:, :, :], tok_dram(x, j)).then_inc(x_loaded, 16)

            def store(b, q):
                if has(b):
                    sp.wait_ge(stored, 16 * b + 16)
                    sp.wait_ge(x3_done, 2 * b + 2 + SEED)
                    sp.dma_start(tok_dram(out, b), xs[q][:, :, :]).then_inc(stored, 16)

            first, end = 3, 7
            for j in range(first):
                load(j, j % 2)
            with sp.Fori(first, end - 1, 2) as j:
                for i in range(2):
                    load(j + i, (first + i) % 2)
                    store(j + i - 3, (first + i - 3) % 2)
            for j in range(end, B + 3):
                load(j, j % 2)
                store(j - 3, (j - 3) % 2)
            sp.wait_ge(stored, 16 * (B + 1))

        @block.tensor
        def _(pe):
            def product32(bank, stationary, moving, first, last):
                return nc.tensor.matmul(bank, stationary, moving, start=first, stop=last)

            def product_split(bank, stationary, moving, first, last):
                (sh, sl), (mh, ml) = stationary, moving
                nc.tensor.matmul(bank, sh, mh, start=first, stop=False)
                nc.tensor.matmul(bank, sh, ml, start=False, stop=False)
                return nc.tensor.matmul(bank, sl, mh, start=False, stop=last)

            def turn(stage, kind, tile, b, j):
                for h in range(CH):
                    take_bank(pe, stage, h, j)
                    if h == 0:
                        pe.wait_ge(normed[kind], b + 1)
                    for t in range(NT):
                        last = nc.tensor.transpose(bank_of(stage, h)[:, t * P:(t + 1) * P], tile[:, t, h * P:(h + 1) * P], ident[:, :])
                    last.then_inc(turned[kind], 1)

            def to_tokens(stage, src, w, done, j):
                for i in range(BANKS):
                    take_bank(pe, stage, i, j)
                    for t in range(TB):
                        tok = (i * TB + t) * P
                        for h in range(CH):
                            last = product32(bank_of(stage, i)[:, t * C:(t + 1) * C], src[:, h, tok:tok + P], w[:, h, :],
                                             h == 0, h == CH - 1)
                    last.then_inc(done, 1)

            def to_channels(bank, src, w, o):
                for h in range(CH):
                    last = product32(bank, w[:, h, o * P:(o + 1) * P], src[:, h, :], h == 0, h == CH - 1)
                return last

            pe.wait_ge(s_gate_rows, 1)
            pe.wait_ge(s_small, 16 * (K + 1))
            nc.tensor.matmul(k_ps[:, 0, 0:C], gate_rows[:, :], bias_sel[:, :], start=True, stop=True).then_inc(s_bias_ps, 1)
            pe.wait_ge(s_const, 3)

            def front_k(f):
                if isinstance(f, int) and f == 0:
                    pe.wait_ge(s_wload["wk"], 16)
                    pe.wait_ge(s_bias, 1)
                pe.wait_ge(xk_done, 2 * f + 2)
                for o in range(CH):
                    reused(pe, z_done, 2 * (f - 1) + o + 1, f)
                    to_channels(k_ps[:, o, :], xk, wk_sb, o).then_inc(kp_ps, 1)

            def front_v(f):
                if isinstance(f, int) and f == 0:
                    pe.wait_ge(s_wload["wv"], 16)
                pe.wait_ge(xv_done, 2 * f + 2)
                for o in range(CH):
                    reused(pe, t1_done, 2 * (f - 1) + o + 1, f)
                    to_channels(v_ps[:, o, :], xv, wv_sb, o).then_inc(vp_ps, 1)

            def front_r(f, j):
                if isinstance(f, int) and f == 0:
                    pe.wait_ge(s_wload["wr"], 16)
                pe.wait_ge(xr_done, 2 * f + 2)
                for o in range(CH):
                    take_bank(pe, "r", o, j)
                    to_channels(bank_of("r", o), dr, wr_sb, o).then_inc(r_ps, 1)

            def channel_keys(e, j):
                if isinstance(e, int) and e == 0 or not isinstance(e, int):
                    pe.wait_ge(s_wck_hi, 1)
                    pe.wait_ge(s_wlo, 1)
                pe.wait_ge(xck_hi_done, 2 * e + 2)
                pe.wait_ge(xck_lo_done, 2 * e + 2)
                for n in range(HB):
                    stage, i = f"kk{n // 2 * 2}", n % 2
                    take_bank(pe, stage, i, j)
                    for h in range(CH):
                        last = product_split(bank_of(stage, i), (wck_hi[:, h, n * P:(n + 1) * P], wck_lo[:, h, n * P:(n + 1) * P]),
                                             (xck_hi[:, h, :], xck_lo[:, h, :]), h == 0, h == CH - 1)
                    last.then_inc(kk_ps, 1)

            def channel_values(e, t, j):
                i, tok = t // TB, t * P
                if t == 0:
                    pe.wait_ge(s_wcv_hi, 1)
                    pe.wait_ge(s_wlo, 2)
                if t % TB == 0:
                    take_bank(pe, "kv", i, j)
                for n in range(HB):
                    if t == 0:
                        pe.wait_ge(*high_done(e, n))
                        pe.wait_ge(*rest_done(e, n))
                    last = product_split(bank_of("kv", i)[:, t % TB * C:(t % TB + 1) * C],
                                         (kk_hi[:, n, tok:tok + P], kk_lo[:, n, tok:tok + P]),
                                         (wcv_hi[:, n, :], wcv_lo[:, n, :]), n == 0, n == HB - 1)
                if t % TB == TB - 1:
                    last.then_inc(kv_ps, 1)

            def step(j, q):
                f, m, e = j, j - 1, j - 2
                if has(e):
                    channel_keys(e, j)
                if has(f):
                    turn("turn_x", "x", norm_x, f, j)
                if has(e):
                    channel_values(e, 0, j)
                    channel_values(e, 1, j)
                if has(f):
                    if isinstance(f, int) and f == 0:
                        pe.wait_ge(s_ffn_acc, K)
                    pe.wait_ge(ffn1_in, 2 * f + 2)
                    to_tokens("y1", ffn_in, ffn_t, y1_ps, j)
                if has(m):
                    if isinstance(m, int) and m == 0:
                        pe.wait_ge(s_wo, 1)
                    pe.wait_ge(rwkv_done, 2 * m + 2)
                    to_tokens("o", rwkv, wo_sb, o_ps, j)
                if has(e):
                    if not isinstance(e, int) or e == 0:
                        pe.wait_ge(s_wload["wcr"], 16)
                    pe.wait_ge(xcr_done, 2 * e + 2)
                    to_tokens("cr", dcr, wcr_sb, cr_ps, j)
                    channel_values(e, 2, j)
                if has(f):
                    turn("turn_x1", "x1", norm_att, f, j)
                if has(e):
                    channel_values(e, 3, j)
                if has(m):
                    turn("turn_xa", "xa", norm_att, m, j)
                if has(f):
                    front_k(f)
                    front_v(f)
                if has(e):
                    turn("turn_x2", "x2", norm_x2, e, j)
                    pe.wait_ge(ffn2_in, 2 * e + 2)
                    to_tokens("y2", ffn_in, ffn_t, y2_ps, j)
                if has(f):
                    front_r(f, j)

            steps(pe, step)

        @block.scalar
        def _(act):
            act.dma_start(gate_col[:, :], gates.rearrange("(k a) -> k a", a=1)).then_inc(s_small, 16)
            act.dma_start(gates_bc[:, :], gates.rearrange("(a k) -> a k", a=1).broadcast_to([P, K])).then_inc(s_gates, 16)
            act.dma_start(vec[:, :, :], vectors).then_inc(s_vec, 16)
            for n, dst, src in (("wr", wr_sb, wr), ("wk", wk_sb, wk), ("wv", wv_sb, wv), ("wo", wo_sb, wo), ("wcr", wcr_sb, wcr),
                                ("wck", wck_raw, wck), ("wcv", wcv_raw, wcv)):
                act.dma_start(dst[:, :, :], src.rearrange("(h p) o -> p h o", p=P)).then_inc(s_wload[n], 16)
            act.wait_ge(s_vec, 16)
            nc.scalar.activation(decay[:, :], V["time_decay"], ACT.Exp).then_inc(s_decay, 1)

            def evac(kind, dst, done, b):
                for h in range(CH):
                    act.wait_ge(turned[kind], 2 * b + h + 1)
                    nc.scalar.activation(dst[:, h, :], bank_of(f"turn_{kind}", h), ACT.Copy).then_inc(done, 1)

            def evac_affine(kind, dst, done, g, off, b):
                for h in range(CH):
                    act.wait_ge(turned[kind], 2 * b + h + 1)
                    nc.scalar.activation(dst[:, h, 1:PAD], bank_of(f"turn_{kind}", h), ACT.Identity,
                                         scale=V[g][:, h:h + 1], bias=V[off][:, h:h + 1]).then_inc(done, 1)

            def key_relu(b, n):
                if n >= KK_BUFS:
                    act.wait_ge(*rest_done(b, n - KK_BUFS))
                act.wait_ge(kk_ps, HB * b + n + 1)
                nc.scalar.activation(kk[:, n % KK_BUFS, :], bank_of(f"kk{n // 2 * 2}", n % 2), ACT.Relu).then_inc(relu_done, 1)

            def key_square(b, n):
                act.wait_ge(relu_done, HB * b + n + 1)
                nc.scalar.activation(kk[:, n % KK_BUFS, :], kk[:, n % KK_BUFS, :], ACT.Square).then_inc(sq_done, 1)

            def key_high(b, n):
                act.wait_ge(sq_done, HB * b + n + 1)
                nc.scalar.activation(kk_hi[:, n, :], kk[:, n % KK_BUFS, :], ACT.Copy).then_inc(high_act, 1)

            def exp_pair(m, src, ready, pos, neg, mid, done):
                for h in range(CH):
                    act.wait_ge(ready, 2 * m + h + 1)
                    nc.scalar.activation(pos[:, h, 0:T], src[:, h, 0:T], ACT.Relu).then_inc(mid, 1)
                    nc.scalar.activation(neg[:, h, 0:T], src[:, h, 0:T], ACT.Relu, scale=-1.0).then_inc(mid, 1)
                for h in range(CH):
                    act.wait_ge(mid, 4 * m + 2 * h + 2)
                    nc.scalar.activation(pos[:, h, 0:T], pos[:, h, 0:T], ACT.Exp, scale=-1.0)
                    nc.scalar.activation(neg[:, h, 0:T], neg[:, h, 0:T], ACT.Exp, scale=-1.0).then_inc(done, 1)

            def step(j, q):
                f, m, e = j, j - 1, j - 2
                if has(e):
                    key_relu(e, 0)
                    for n in range(HB):
                        if n + 1 < HB:
                            key_relu(e, n + 1)
                        key_square(e, n)
                        if n in ACT_HIGHS:
                            key_high(e, n)
                if has(m):
                    act.preload_act_table_set("natural_log_exp_and_others")
                    for h in range(CH):
                        act.wait_ge(den_done, 2 * m + h + 1)
                        nc.scalar.activation(eb_v[:, h, 0:T], e_v[:, h, 0:T], ACT.Ln).then_inc(ln_done, 1)
                    for h in range(CH):
                        act.wait_ge(ln_done, 2 * m + h + 1)
                        nc.scalar.activation(eb_v[:, h, 0:T], eb_v[:, h, 0:T], ACT.Exp, scale=-1.0).then_inc(r0_done, 1)
                if has(f):
                    evac("x", ffn_in, ffn1_in, f)
                if has(e):
                    for i in range(BANKS):
                        act.wait_ge(cr_ps, 2 * e + i + 1)
                        nc.scalar.activation(tok_bank(thc, i), bank3(bank_of("cr", i)), ACT.Tanh, scale=0.5).then_inc(thc_done, 1)
                if has(f):
                    evac_affine("x1", h1, h1_done, "ln1_g", "ln1_b", f)
                if has(m):
                    evac_affine("xa", h2, h2_done, "ln2_g", "ln2_b", m)
                    for h in range(CH):
                        act.wait_ge(xck_done, 2 * m + h + 1)
                        nc.scalar.activation(xck_hi[:, h, :], xck[:, h, :], ACT.Copy).then_inc(xck_hi_done, 1)
                if has(e):
                    evac("x2", ffn_in, ffn2_in, e)
                if has(f):
                    exp_pair(f, z2, z2_done, eb_v, eb_s, rect2, eb_done)
                    exp_pair(f, z, z_done, e_s, e_v, rect, e_done)
                    for h in range(CH):
                        act.wait_ge(r_ps, 2 * f + h + 1)
                        nc.scalar.activation(thr[:, h, :], bank_of("r", h), ACT.Tanh, scale=0.5).then_inc(thr_done, 1)

            steps(act, step)

        @block.vector
        def _(dve):
            dve.sem_inc(x3_done, SEED)
            dve.wait_ge(s_decay, 1)
            nc.vector.tensor_scalar(decay[:, :], decay[:, :], -1.0, None, ALU.mult).then_inc(s_decay_neg, 1)
            dve.wait_ge(s_small, 16 * (K + 1))
            dve.wait_ge(s_const, 2)
            nc.vector.tensor_scalar(gate_rows[:, :], gate_rows[:, :], gate_col[:, 0:1], 0.5, ALU.mult, ALU.mult).then_inc(s_gate_rows, 1)
            dve.wait_ge(s_gates, 16)
            nc.vector.tensor_scalar(gates_bc[:, :], gates_bc[:, :], 0.5, None, ALU.mult).then_inc(s_gates, 1)

            def stats(kind, tile, b):
                for t in range(NT):
                    last = nc.vector.bn_stats(bn[kind][:, t, :], tile[:, t, :])
                last.then_inc(bn_done[kind], 1)
                dve.wait_ge(bn_done[kind], b + 1)
                own_wait(nc.vector, b)
                for t in range(NT):
                    last = nc.vector.bn_aggr(mv[kind][:, t, :], bn[kind][:, t, :])
                last.then_inc(mv_done[kind], 1)

            def ffn_weights():
                dve.wait_ge(s_gates, 17)
                dve.wait_ge(s_sel, 16 * K)
                for k in range(K):
                    g = gates_bc[:, k:k + 1]
                    if k == 0:
                        nc.vector.tensor_scalar(ffn_t[:, :, :], sel[:, 0, :, :], g, None, ALU.mult).then_inc(s_ffn_acc, 1)
                    else:
                        dve.wait_ge(s_ffn_acc, k)
                        nc.vector.scalar_tensor_tensor(ffn_t[:, :, :], sel[:, k, :, :], g, ffn_t[:, :, :], ALU.mult, ALU.add).then_inc(s_ffn_acc, 1)
                dve.wait_ge(s_bias_ps, 1)
                nc.vector.tensor_copy(bias_bc[:, :], k_ps[:, 0, 0:C]).then_inc(s_bias, 1)

            def other_weights():
                dve.wait_ge(s_wload["wo"], 16)
                nc.vector.tensor_scalar(wo_sb[:, :, :], wo_sb[:, :, :], 0.5, None, ALU.mult).then_inc(s_wo, 1)
                dve.wait_ge(s_wload["wck"], 16)
                nc.vector.tensor_copy(wck_hi[:, :, :], wck_raw).then_inc(s_wck_hi, 1)
                dve.wait_ge(s_wload["wcv"], 16)
                nc.vector.tensor_scalar(wcv_raw, wcv_raw, 0.5, None, ALU.mult).then_inc(s_wcv_half, 1)
                dve.wait_ge(s_wck_hi, 1)
                nc.vector.tensor_tensor(wck_lo[:, :, :], wck_raw, wck_hi[:, :, :].bitcast(F32), ALU.subtract).then_inc(s_wlo, 1)
                dve.wait_ge(s_wcv_half, 1)
                nc.vector.tensor_copy(wcv_hi[:, :, :], wcv_raw).then_inc(s_wcv_hi, 1)
                dve.wait_ge(s_wcv_hi, 1)
                nc.vector.tensor_tensor(wcv_lo[:, :, :], wcv_raw, wcv_hi[:, :, :].bitcast(F32), ALU.subtract).then_inc(s_wlo, 1)
                dve.wait_ge(s_wlo, 2)
                nc.vector.memset(pp[:, :, 0:1], NEG)
                nc.vector.memset(aa[:, :, 0:1], 0.0)
                nc.vector.memset(bb[:, :, 0:1], 0.0).then_inc(s_pads, 1)

            def wkv_exponents(m):
                for h in range(CH):
                    dve.wait_ge(kp_ps, 2 * m + h + 1)
                    nc.vector.tensor_tensor_scan(pp[:, h, 1:PAD], decay[:, h:h + 1].to_broadcast([P, T]), k_ps[:, h, :],
                                                 NEG, ALU.add, ALU.max).then_inc(pp_done, 1)
                for h in range(CH):
                    dve.wait_ge(pp_done, 2 * m + h + 1)
                    nc.vector.scalar_tensor_tensor(z2[:, h, 0:T], pp[:, h, 0:T], decay[:, h:h + 1], k_ps[:, h, :],
                                                   ALU.add, ALU.subtract).then_inc(z2_done, 1)
                for h in range(CH):
                    nc.vector.scalar_tensor_tensor(z[:, h, 0:T], k_ps[:, h, :], V["time_first"][:, h:h + 1], pp[:, h, 0:T],
                                                   ALU.add, ALU.subtract).then_inc(z_done, 1)

            def wkv_terms(m):
                for h in range(CH):
                    dve.wait_ge(e_done, 2 * m + h + 1)
                    nc.vector.tensor_tensor(z[:, h, 0:T], e_v[:, h, 0:T], v_ps[:, h, :], ALU.mult).then_inc(t1_done, 1)

            def wkv_states(m):
                for h in range(CH):
                    dve.wait_ge(eb_done, 2 * m + h + 1)
                    nc.vector.tensor_tensor_scan(bb[:, h, 1:PAD], eb_s[:, h, 0:T], eb_v[:, h, 0:T], 0.0, ALU.mult, ALU.add).then_inc(bb_done, 1)
                    dve.wait_ge(vp_ps, 2 * m + h + 1)
                    nc.vector.tensor_tensor(z2[:, h, 0:T], eb_v[:, h, 0:T], v_ps[:, h, :], ALU.mult).then_inc(ev_done, 1)
                for h in range(CH):
                    dve.wait_ge(ev_done, 2 * m + h + 1)
                    nc.vector.tensor_tensor_scan(aa[:, h, 1:PAD], eb_s[:, h, 0:T], z2[:, h, 0:T], 0.0, ALU.mult, ALU.add).then_inc(aa_done, 1)

            def wkv_denominator(m):
                for h in range(CH):
                    dve.wait_ge(t3_done, 2 * m + h + 1)
                    nc.vector.tensor_tensor(e_v[:, h, 0:T], e_v[:, h, 0:T], eb_v[:, h, 0:T], ALU.add).then_inc(den_done, 1)

            def wkv_numerator(m):
                for h in range(CH):
                    dve.wait_ge(t2_done, 2 * m + h + 1)
                    dve.wait_ge(t1_done, 2 * m + h + 1)
                    nc.vector.tensor_tensor(z[:, h, 0:T], z[:, h, 0:T], z2[:, h, 0:T], ALU.add).then_inc(num_done, 1)

            def wkv_reciprocal(m):
                for h in range(CH):
                    dve.wait_ge(dr0_done, 2 * m + h + 1)
                    nc.vector.scalar_tensor_tensor(eb_s[:, h, 0:T], eb_s[:, h, 0:T], 2.0, eb_v[:, h, 0:T], ALU.subtract, ALU.mult,
                                                   reverse0=True).then_inc(rec_done, 1)

            def wkv_quotient(m):
                for h in range(CH):
                    dve.wait_ge(rec_done, 2 * m + h + 1)
                    dve.wait_ge(num_done, 2 * m + h + 1)
                    nc.vector.tensor_tensor(z[:, h, 0:T], z[:, h, 0:T], eb_s[:, h, 0:T], ALU.mult).then_inc(y_done, 1)

            def wkv_gate(m):
                for h in range(CH):
                    dve.wait_ge(y_done, 2 * m + h + 1)
                    dve.wait_ge(thr_done, 2 * m + h + 1)
                    nc.vector.scalar_tensor_tensor(rwkv[:, h, :], thr[:, h, :], 1.0, z[:, h, 0:T], ALU.add, ALU.mult).then_inc(rwkv_done, 1)

            def key_high(e, n):
                dve.wait_ge(sq_done, HB * e + n + 1)
                nc.vector.tensor_copy(kk_hi[:, n, :], kk[:, n % KK_BUFS, :]).then_inc(high_dve, 1)

            def value_sum(e, i, q):
                dve.wait_ge(kv_ps, 2 * e + i + 1)
                dve.wait_ge(thc_done, 2 * e + i + 1)
                nc.vector.scalar_tensor_tensor(tok_bank(thc, i), tok_bank(thc, i), 1.0, bank3(bank_of("kv", i)), ALU.add, ALU.mult).then_inc(kvs_done, 1)
                dve.wait_ge(kvs_done, 2 * e + i + 1)
                dve.wait_ge(xs_done, e + 1)
                nc.vector.tensor_tensor(tok_bank(xs[q], i), tok_bank(xs[q], i), tok_bank(thc, i), ALU.add).then_inc(x2_done, 1)

            def mix(dst, d, h, prev, m, done):
                for c in range(CH):
                    nc.vector.scalar_tensor_tensor(dst[:, c, :], d[:, c, :], V[m][:, c:c + 1], h[:, c, prev:prev + T],
                                                   ALU.mult, ALU.add).then_inc(done, 1)

            def difference(dst, h, ready, b, done):
                for c in range(CH):
                    dve.wait_ge(ready, 2 * b + c + 1)
                    nc.vector.tensor_tensor(dst[:, c, :], h[:, c, 1:PAD], h[:, c, 0:T], ALU.subtract).then_inc(done, 1)
                dve.wait_ge(done, 2 * b + 2)

            def step(j, q):
                f, m, e = j, j - 1, j - 2
                if has(f):
                    dve.wait_ge(x_loaded, 16 * f + 16)
                    stats("x", x1[q], f)
                if isinstance(j, int) and j == 0:
                    ffn_weights()
                if has(m):
                    wkv_states(m)
                if has(e):
                    key_high(e, 1)
                    key_rest(nc.vector, dve, e, 0)
                if has(m):
                    wkv_terms(m)
                if has(e):
                    key_high(e, 3)
                    key_rest(nc.vector, dve, e, 2)
                if has(m):
                    wkv_denominator(m)
                if has(e):
                    key_high(e, 5)
                    key_rest(nc.vector, dve, e, 4)
                    for n in (6, 7):
                        key_high(e, n)
                        key_rest(nc.vector, dve, e, n)
                if has(m):
                    wkv_numerator(m)
                    wkv_reciprocal(m)
                    wkv_quotient(m)
                    wkv_gate(m)
                if has(f):
                    for i in range(BANKS):
                        dve.wait_ge(y1_ps, 2 * f + i + 1)
                        dve.wait_ge(xb_done, f + 1)
                        nc.vector.tensor_tensor(tok_bank(x1[q], i), tok_bank(x1[q], i), bank3(bank_of("y1", i)), ALU.add).then_inc(x1_done, 1)
                    dve.wait_ge(x1_done, 2 * f + 2)
                    stats("x1", x1[q], f)
                if has(m):
                    for i in range(BANKS):
                        dve.wait_ge(o_ps, 2 * m + i + 1)
                        dve.wait_ge(xa_done, m + 1)
                        nc.vector.tensor_tensor(tok_bank(xa, i), tok_bank(xa, i), bank3(bank_of("o", i)), ALU.add).then_inc(xa2_done, 1)
                    dve.wait_ge(xa2_done, 2 * m + 2)
                    stats("xa", xa, m)
                if isinstance(j, int) and j == 0:
                    other_weights()
                    dve.wait_ge(s_pads, 1)
                if has(e):
                    value_sum(e, 0, q)
                if has(f):
                    difference(dr, h1, h1_done, f, d1_done)
                    mix(xk, dr, h1, 0, "tm_k", xk_done)
                if has(e):
                    value_sum(e, 1, q)
                    dve.wait_ge(x2_done, 2 * e + 2)
                    stats("x2", xs[q], e)
                if has(f):
                    mix(xv, dr, h1, 0, "tm_v", xv_done)
                if has(m):
                    difference(dcr, h2, h2_done, m, d2_done)
                    mix(xck, dcr, h2, 0, "cm_k", xck_done)
                if has(f):
                    wkv_exponents(f)
                    mix(dr, dr, h1, 0, "tm_r", xr_done)
                if has(m):
                    mix(dcr, dcr, h2, 0, "cm_r", xcr_done)
                if has(e):
                    for i in range(BANKS):
                        dve.wait_ge(y2_ps, 2 * e + i + 1)
                        dve.wait_ge(x2b_done, e + 1)
                        nc.vector.tensor_tensor(tok_bank(xs[q], i), tok_bank(xs[q], i), bank3(bank_of("y2", i)), ALU.add).then_inc(x3_done, 1)

            steps(dve, step)

        @block.gpsimd
        def _(pool):
            nc.gpsimd.memset(ident[:, :], 0.0).then_inc(s_const, 1)
            nc.gpsimd.memset(gate_rows[:, :], 1.0).then_inc(s_const, 1)
            pool.wait_ge(s_const, 1)
            nc.gpsimd.affine_select(out=ident[:, :], in_=ident[:, :], compare_op=ALU.not_equal, fill=1.0, base=0,
                                    pattern=[[-1, P]], channel_multiplier=1).then_inc(s_const, 1)
            nc.gpsimd.memset(nhalf[:, :], -0.5)
            nc.gpsimd.memset(minus[:, :], -1.0)
            nc.gpsimd.memset(eps[:, :], EPS)
            nc.gpsimd.memset(eps_sq[:, :], EPS * EPS)
            nc.gpsimd.memset(one_eps[:, :], 1.0 + EPS)
            nc.gpsimd.memset(h1[:, :, 0:1], 0.0)
            nc.gpsimd.memset(h2[:, :, 0:1], 0.0).then_inc(s_const, 1)
            pool.wait_ge(s_const, 4)

            def inverse_std(kind, b):
                pool.wait_ge(mv_done[kind], b + 1)
                nc.gpsimd.tensor_tensor(vare[kind][:, :], mv[kind][:, :, 1], eps[:, :], ALU.add).then_inc(rs_steps[kind], 1)
                nc.gpsimd.tensor_tensor(negm[kind][:, :], mv[kind][:, :, 0], minus[:, :], ALU.mult).then_inc(rs_steps[kind], 1)
                pool.wait_ge(rs_steps[kind], 3 * b + 1)
                nc.gpsimd.tensor_tensor(rstd[kind][:, :], vare[kind][:, :], nhalf[:, :], ALU.pow).then_inc(rs_steps[kind], 1)
                pool.wait_ge(rs_steps[kind], 3 * b + 3)
                own_wait(nc.gpsimd, b)

            def double_inverse_std(f):
                k, c = "x1", 4 * f
                pool.wait_ge(mv_done[k], f + 1)
                nc.gpsimd.tensor_tensor(both[:, :], mv[k][:, :, 1], one_eps[:, :], ALU.mult).then_inc(rs_steps[k], 1)
                nc.gpsimd.tensor_tensor(negm[k][:, :], mv[k][:, :, 0], minus[:, :], ALU.mult).then_inc(rs_steps[k], 1)
                pool.wait_ge(rs_steps[k], c + 1)
                nc.gpsimd.tensor_tensor(both[:, :], both[:, :], eps_sq[:, :], ALU.add).then_inc(rs_steps[k], 1)
                pool.wait_ge(rs_steps[k], c + 3)
                nc.gpsimd.tensor_tensor(rboth[:, :], both[:, :], nhalf[:, :], ALU.pow).then_inc(rs_steps[k], 1)
                pool.wait_ge(rs_steps[k], c + 4)
                own_wait(nc.gpsimd, f)

            def single_inverse_std(f):
                nc.gpsimd.tensor_tensor(vare["x1"][:, :], mv["x1"][:, :, 1], eps[:, :], ALU.add).then_inc(rs1_steps, 1)
                pool.wait_ge(rs1_steps, 2 * f + 1)
                nc.gpsimd.tensor_tensor(rstd["x1"][:, :], vare["x1"][:, :], nhalf[:, :], ALU.pow).then_inc(rs1_steps, 1)
                pool.wait_ge(rs1_steps, 2 * f + 2)
                own_wait(nc.gpsimd, f)

            def centre_scale(dst, src, kind, scale, done):
                for t in range(NT):
                    last = nc.gpsimd.tensor_scalar(dst[:, t, :], src[:, t, :], negm[kind][:, t:t + 1], scale[:, t:t + 1], ALU.add, ALU.mult)
                last.then_inc(done, 1)

            def add_bias(tile, done):
                last = nc.gpsimd.tensor_tensor(tile, tile, bias_bc[:, :].rearrange("p (a c) -> p a c", a=1).broadcast_to([P, NT, C]), ALU.add)
                last.then_inc(done, 1)

            def step(j, q):
                f, m, e = j, j - 1, j - 2
                if has(f):
                    inverse_std("x", f)
                    centre_scale(norm_x, x1[q], "x", rstd["x"], normed["x"])
                if has(m):
                    for h in range(CH):
                        pool.wait_ge(bb_done, 2 * m + h + 1)
                        pool.wait_ge(e_done, 2 * m + h + 1)
                        pool.wait_ge(ev_done, 2 * m + h + 1)
                        nc.gpsimd.tensor_tensor(eb_v[:, h, 0:T], e_s[:, h, 0:T], bb[:, h, 0:T], ALU.mult).then_inc(t3_done, 1)
                if has(e):
                    for n in POOL_RESTS[:2]:
                        key_rest(nc.gpsimd, pool, e, n)
                if has(m):
                    for h in range(CH):
                        pool.wait_ge(aa_done, 2 * m + h + 1)
                        nc.gpsimd.tensor_tensor(z2[:, h, 0:T], e_s[:, h, 0:T], aa[:, h, 0:T], ALU.mult).then_inc(t2_done, 1)
                if has(e):
                    for n in POOL_RESTS[2:]:
                        key_rest(nc.gpsimd, pool, e, n)
                if has(f):
                    if isinstance(f, int) and f == 0:
                        pool.wait_ge(s_bias, 1)
                    pool.wait_ge(normed["x"], f + 1)
                    add_bias(x1[q][:, :, :], xb_done)
                if has(m):
                    for h in range(CH):
                        pool.wait_ge(r0_done, 2 * m + h + 1)
                        nc.gpsimd.tensor_tensor(eb_s[:, h, 0:T], e_v[:, h, 0:T], eb_v[:, h, 0:T], ALU.mult).then_inc(dr0_done, 1)
                if has(f):
                    double_inverse_std(f)
                    centre_scale(norm_att, x1[q], "x1", rboth, normed["x1"])
                if has(m):
                    inverse_std("xa", m)
                    if has(f):
                        pool.wait_ge(turned["x1"], 2 * f + 2)
                        own_wait(nc.gpsimd, f)
                    centre_scale(norm_att, xa, "xa", rstd["xa"], normed["xa"])
                    if not (isinstance(m, int) and m < 2):
                        pool.wait_ge(stored, 16 * (m - 1) + 16)
                    nc.gpsimd.tensor_tensor(xs[1 - q][:, :, :], x1[1 - q][:, :, :], xa[:, :, :], ALU.add).then_inc(xs_done, 1)
                if has(e):
                    inverse_std("x2", e)
                    centre_scale(norm_x2, xs[q], "x2", rstd["x2"], normed["x2"])
                if has(m):
                    for h in range(CH):
                        pool.wait_ge(xck_hi_done, 2 * m + h + 1)
                        nc.gpsimd.tensor_tensor(xck_lo[:, h, :], xck[:, h, :], xck_hi[:, h, :].bitcast(F32), ALU.subtract).then_inc(xck_lo_done, 1)
                if has(e):
                    pool.wait_ge(normed["x2"], e + 1)
                    add_bias(xs[q][:, :, :], x2b_done)
                if has(f):
                    single_inverse_std(f)
                    centre_scale(xa, x1[q], "x1", rstd["x1"], xa_done)

            steps(pool, step)


_INS = ["x", "ffn_w", "ffn_b", "ids", "gates", "vectors", "wk", "wv", "wr", "wo", "wcr", "wck", "wcv"]


def kernel(**inputs):
    import numpy as _np
    import concourse.bacc as _bacc
    from concourse import mybir as _mybir
    from concourse.bass_utils import run_bass_kernel_spmd as _run

    def given(name):
        return _np.asarray(inputs[name])

    def turned(name):
        return given(name).T

    laid = {
        "x": given("L0_attn_x"),
        "ffn_w": given("L0_ffn_W").transpose(0, 2, 1),
        "ffn_b": given("L0_ffn_b"),
        "ids": given("L0_ffn_ids"),
        "gates": given("L0_ffn_weights"),
        "vectors": _np.stack([given(f"L0_attn_{n}").reshape(-1, P) for n in VECTORS]).transpose(2, 0, 1),
        "wk": turned("L0_attn_Wk"), "wv": turned("L0_attn_Wv"), "wr": turned("L0_attn_Wr"), "wo": turned("L0_attn_Wo"),
        "wcr": turned("L0_attn_Wcr"), "wck": turned("L0_attn_Wck"), "wcv": turned("L0_attn_Wcv"),
    }
    nc = _bacc.Bacc("TRN2", target_bir_lowering=False, num_devices=1)
    arrays, args = {}, []
    for name in _INS:
        a = _np.ascontiguousarray(laid[name])
        arrays[f"in_{name}_dram"] = a
        args.append(nc.dram_tensor(f"in_{name}_dram", a.shape, _mybir.dt.from_np(a.dtype), kind="ExternalInput").ap())
    shape = laid["x"].shape
    args.append(nc.dram_tensor("out_0_dram", shape, _mybir.dt.from_np(_np.dtype("float32")), kind="ExternalOutput").ap())
    build(nc, *args)
    r = _run(nc, [arrays], core_ids=[0])
    return r.results[0]["out_0_dram"]
```

```python
from contextlib import ExitStack

import concourse.bass as bass
from concourse import mybir

ALU = mybir.AluOpType
ACT = mybir.ActivationFunctionType
F32 = mybir.dt.float32
F32R = mybir.dt.float32r

P = 128
EPS = 1e-5
NEG = -1e38
VECTORS = ["ln1_g", "ln1_b", "ln2_g", "ln2_b", "time_decay", "time_first", "tm_k", "tm_v", "tm_r", "cm_k", "cm_r"]


def build(nc, x, ffn_w, ffn_b, ids, gates, vectors, wk, wv, wr, wo, wcr, wck, wcv, out):
    B, T, C = x.shape
    HID = wck.shape[1]
    K = ids.shape[0]
    N_ADAPTERS = ffn_w.shape[0]
    CH = C // P
    NT = T // P
    HB = HID // P
    BANKS = 2
    TB = NT // BANKS
    KK_BUFS = 4
    ACT_HIGHS = (0,)
    POOL_RESTS = (3, 5)
    LAG = 2
    PAD = T + 1

    with ExitStack() as ctx:
        def sb(name, shape, dt=F32):
            return ctx.enter_context(nc.sbuf_tensor(name, shape, dt))

        def sem(name):
            return ctx.enter_context(nc.semaphore(name))

        ident = sb("ident", [P, P])
        vec = sb("vec", [P, len(VECTORS), CH])
        V = {n: vec[:, i, :] for i, n in enumerate(VECTORS)}
        decay = sb("decay", [P, CH])
        nhalf = sb("nhalf", [P, NT])
        minus = sb("minus", [P, NT])
        eps = sb("eps", [P, NT])
        eps_sq = sb("eps_sq", [P, NT])
        one_eps = sb("one_eps", [P, NT])
        carried = sb("carried", [P, 32])
        gates_bc = sb("gates_bc", [P, K])
        gate_col = sb("gate_col", [K, 1])
        gate_rows = sb("gate_rows", [K, P])
        bias_sel = sb("bias_sel", [K, C])
        bias_bc = sb("bias_bc", [P, C])
        ids_row = sb("ids_row", [1, K], ids.dtype)
        ffn_t = sb("ffn_t", [P, CH, C])
        wr_sb, wo_sb = sb("wr_sb", [P, CH, C]), sb("wo_sb", [P, CH, C])
        wk_hi, wk_lo, wv_hi, wv_lo, wcr_hi, wcr_lo = (
            sb(n, [P, CH, C], F32R) for n in ("wk_hi", "wk_lo", "wv_hi", "wv_lo", "wcr_hi", "wcr_lo"))
        wck_hi = sb("wck_hi", [P, CH, HID], F32R)
        wck_lo = sb("wck_lo", [P, CH, HID], F32R)
        wcv_hi = sb("wcv_hi", [P, HB, C], F32R)
        wcv_lo = sb("wcv_lo", [P, HB, C], F32R)

        x1 = [sb(f"x1_{i}", [P, NT, C]) for i in range(2)]
        xs = [sb(f"xs_{i}", [P, NT, C]) for i in range(2)]
        norm = sb("norm", [P, NT, C])
        xa = sb("xa", [P, NT, C])
        thc = sb("thc", [P, NT, C])
        kinds = ("x", "x1", "xa", "x2")
        bn = {k: sb(f"bn_{k}", [P, NT, 6]) for k in kinds}
        mv = {k: sb(f"mv_{k}", [P, NT, 2]) for k in kinds}
        negm = {k: sb(f"negm_{k}", [P, NT]) for k in kinds}
        vare = {k: sb(f"vare_{k}", [P, NT]) for k in kinds}
        rstd = {k: sb(f"rstd_{k}", [P, NT]) for k in kinds}
        both = sb("both", [P, NT])
        shift_x2 = sb("shift_x2", [P, NT])
        rboth = sb("rboth", [P, NT])

        ffn_in = sb("ffn_in", [P, CH, T])
        h1 = sb("h1", [P, CH, PAD])
        h2 = sb("h2", [P, CH, PAD])
        dr = sb("dr", [P, CH, T])
        dcr = sb("dcr", [P, CH, T])
        xk_hi = xck_hi = sb("x_key_hi", [P, CH, T], F32R)
        xk_lo = xck_lo = sb("x_key_lo", [P, CH, T], F32R)
        xv_hi = xcr_hi = sb("x_value_hi", [P, CH, T], F32R)
        xv_lo = xcr_lo = sb("x_value_lo", [P, CH, T], F32R)
        kk = sb("kk", [P, KK_BUFS, T])
        kk_hi = sb("kk_hi", [P, HB, T], F32R)
        kk_lo = sb("kk_lo", [P, HB, T], F32R)
        thr = sb("thr", [P, CH, T])
        rwkv = sb("rwkv", [P, CH, T])
        xck = rwkv
        work = sb("work", [P, 9 * CH * PAD])
        pp, aa, bb, z2, z, eb_v, eb_s, e_s, e_v = (
            work[:, i * CH * PAD:(i + 1) * CH * PAD].rearrange("p (h t) -> p h t", h=CH) for i in range(9))
        xk, xv = z2[:, :, 0:T], z[:, :, 0:T]
        sel = work[:, 0:K * CH * C].rearrange("p (k h o) -> p k h o", k=K, h=CH)
        assert K * CH * C <= 9 * CH * PAD
        wck_raw = kk[:, :, :].rearrange("p n t -> p (n t)").rearrange("p (h o) -> p h o", h=CH)
        wk_raw, wv_raw = (xs[0][:, i * CH:(i + 1) * CH, :] for i in range(2))
        wcr_raw = xs[1][:, 0:CH, :]
        wcv_raw = [thc[:, :, :], dcr[:, :, :].rearrange("p h t -> p (h t)").rearrange("p (n o) -> p n o", n=NT)]
        assert CH * HID == KK_BUFS * T and HB == 2 * NT

        k_ps = ctx.enter_context(nc.psum_tensor("k_ps", [P, CH, T], F32))
        v_ps = ctx.enter_context(nc.psum_tensor("v_ps", [P, CH, T], F32))
        ring = [ctx.enter_context(nc.psum_tensor(f"ring{i}", [P, T], F32)) for i in range(4)]

        s_const, s_vec, s_small, s_ids, s_bias_sel, s_pads = (
            sem(n) for n in ("s_const", "s_vec", "s_small", "s_ids", "s_bias_sel", "s_pads"))
        s_sel = [sem(f"s_sel_{k}") for k in range(K)]
        s_wload = {n: sem(f"s_load_{n}") for n in ("wk", "wv", "wr", "wo", "wcr", "wck", "wcv")}
        s_decay, s_decay_neg, s_gates = (sem(n) for n in ("s_decay", "s_decay_neg", "s_gates"))
        s_gate_rows, s_bias_ps, s_bias, s_ffn_acc = (sem(n) for n in ("s_gate_rows", "s_bias_ps", "s_bias", "s_ffn_acc"))
        s_wo, s_wcv_half, s_wck_hi, s_wcv_hi, s_wlo = (sem(n) for n in ("s_wo", "s_wcv_half", "s_wck_hi", "s_wcv_hi", "s_wlo"))
        x_loaded, stored = sem("x_loaded"), sem("stored")
        bn_done = {k: sem(f"bn_done_{k}") for k in kinds}
        mv_done = {k: sem(f"mv_done_{k}") for k in kinds}
        rs_steps = {k: sem(f"rs_steps_{k}") for k in kinds}
        normed = {k: sem(f"normed_{k}") for k in kinds}
        rs1_steps = sem("rs1_steps")
        shift_done, normed_act = sem("shift_done"), sem("normed_act")
        xa_done, xb_done, x2b_done, xs_done = (sem(n) for n in ("xa_done", "xb_done", "x2b_done", "xs_done"))
        turned = {k: sem(f"turned_{k}") for k in kinds}
        ffn1_in, ffn2_in, h1_done, h2_done = (sem(n) for n in ("ffn1_in", "ffn2_in", "h1_done", "h2_done"))
        d1_done, d2_done = sem("d1_done"), sem("d2_done")
        xk_done, xv_done, xr_done, xck_done, xcr_done = (sem(n) for n in ("xk_done", "xv_done", "xr_done", "xck_done", "xcr_done"))
        xck_hi_done, xck_lo_done = sem("xck_hi_done"), sem("xck_lo_done")
        xk_hi_done, xk_lo_done, xv_hi_done, xv_lo_done, xcr_hi_done, xcr_lo_done = (
            sem(n) for n in ("xk_hi_done", "xk_lo_done", "xv_hi_done", "xv_lo_done", "xcr_hi_done", "xcr_lo_done"))
        s_small_hi, s_small_lo = sem("s_small_hi"), sem("s_small_lo")
        y1_ps, y2_ps, o_ps, r_ps, kp_ps, vp_ps, cr_ps, kk_ps, kv_ps = (
            sem(n) for n in ("y1_ps", "y2_ps", "o_ps", "r_ps", "kp_ps", "vp_ps", "cr_ps", "kk_ps", "kv_ps"))
        x1_done, xa2_done, kvs_done, x2_done, x3_done = (sem(n) for n in ("x1_done", "xa2_done", "kvs_done", "x2_done", "x3_done"))
        thr_done, thc_done = sem("thr_done"), sem("thc_done")
        relu_done, sq_done = sem("relu_done"), sem("sq_done")
        high_act, high_dve = sem("high_act"), sem("high_dve")
        rest_pool, rest_dve = sem("rest_pool"), sem("rest_dve")
        pp_done, z2_done, z_done, rect2, rect, eb_done, e_done = (
            sem(n) for n in ("pp_done", "z2_done", "z_done", "rect2", "rect", "eb_done", "e_done"))
        bb_done, ev_done, aa_done, t1_done, t2_done, t3_done, den_done = (
            sem(n) for n in ("bb_done", "ev_done", "aa_done", "t1_done", "t2_done", "t3_done", "den_done"))
        ln_done, r0_done, dr0_pool, dr0_dve, rec_done, num_done, gated_done, rwkv_done = (
            sem(n) for n in ("ln_done", "r0_done", "dr0_pool", "dr0_dve", "rec_done", "num_done", "gated_done", "rwkv_done"))

        last_mv, last_steps_rs, last_shift, last_normed_pool, last_normed_act, last_turned, last_in, last_bias = (
            sem(n) for n in ("last_mv", "last_steps_rs", "last_shift", "last_normed_pool", "last_normed_act", "last_turned", "last_in",
                             "last_bias"))

        SEED = 2

        def pair(s, seed=0):
            return lambda b, i: (s, seed + 2 * b + i + 1)

        def keys_read(n):
            return lambda b, i: (relu_done, HB * b + n + i + 1)

        LOW = [("kk0", -2, keys_read(0)), ("kk4", -2, keys_read(4)), ("turn_x", 0, pair(ffn1_in)), ("y1", 0, pair(x1_done)),
               ("o", -1, pair(xa2_done)), ("cr", -2, pair(thc_done)), ("turn_x1", 0, pair(h1_done)), ("turn_xa", -1, pair(h2_done)),
               ("r", 0, pair(thr_done))]
        HIGH = [("kk2", -2, keys_read(2)), ("kk6", -2, keys_read(6)), ("kv", -2, pair(kvs_done)), ("turn_x2", -2, pair(ffn2_in)),
                ("y2", -2, pair(x3_done, SEED))]

        def bank_of(stage, i):
            return ring[i if any(u[0] == stage for u in LOW) else 2 + i][:, :]

        def reader_before(order, at, step, i):
            at -= 1
            if at < 0:
                at, step = len(order) - 1, step - 1
            _, rel, last_read = order[at]
            return last_read(step + rel, i)

        taken = {}

        def take_bank(pe, stage, i, b):
            order = LOW if any(u[0] == stage for u in LOW) else HIGH
            at = [u[0] for u in order].index(stage)
            _, rel, last_read = order[at]
            if not isinstance(b, int):
                pe.wait_ge(*reader_before(order, at, b - rel, i))
                taken.clear()
                return
            key = (order is LOW, i)
            if key in taken:
                pe.wait_ge(*taken[key])
            elif b - rel >= B:
                pe.wait_ge(*reader_before(order, 0, B, i))
            taken[key] = last_read(b, i)

        def reused(eng, s, count, b):
            if not isinstance(b, int) or b > 0:
                eng.wait_ge(s, count)

        def has(b):
            return not isinstance(b, int) or 0 <= b < B

        def high_done(b, n):
            mine = [i for i in range(HB) if (i in ACT_HIGHS) == (n in ACT_HIGHS)]
            return (high_act if n in ACT_HIGHS else high_dve), len(mine) * b + mine.index(n) + 1

        def rest_done(b, n):
            mine = [i for i in range(HB) if (i in POOL_RESTS) == (n in POOL_RESTS)]
            return (rest_pool if n in POOL_RESTS else rest_dve), len(mine) * b + mine.index(n) + 1

        def key_rest(engine, eng, b, n):
            eng.wait_ge(*high_done(b, n))
            engine.tensor_tensor(kk_lo[:, n, :], kk[:, n % KK_BUFS, :], kk_hi[:, n, :].bitcast(F32), ALU.subtract).then_inc(rest_done(b, n)[0], 1)

        def rest(engine, eng, dst, hi, src, ready, done, b):
            for h in range(CH):
                eng.wait_ge(ready, 2 * b + h + 1)
                engine.tensor_tensor(dst[:, h, :], src[:, h, :], hi[:, h, :].bitcast(F32), ALU.subtract).then_inc(done, 1)

        def key_input_rest(engine, eng, m):
            rest(engine, eng, xck_lo, xck_hi, xck, xck_hi_done, xck_lo_done, m)

        def gate_input_rest(engine, eng, m):
            rest(engine, eng, xcr_lo, xcr_hi, dcr, xcr_hi_done, xcr_lo_done, m)

        def load_adapters(queue, numbers):
            queue.wait_ge(s_ids, 16)
            for k in numbers:
                v = queue.value_load(ids_row[0:1, k:k + 1], min_val=0, max_val=N_ADAPTERS - 1)
                queue.dma_start(sel[:, k, :, :], ffn_w[v, :, :].rearrange("(h p) o -> p h o", p=P)).then_inc(s_sel[k], 16)
                queue.dma_start(bias_sel[k:k + 1, :], ffn_b[v, :].rearrange("(a c) -> a c", a=1)).then_inc(s_bias_sel, 16)

        def last_bank(i):
            return ring[i][:, :].rearrange("p (h t) -> p h t", h=CH)

        carriers = []

        def own_wait(engine, b):
            if not isinstance(b, int):
                at = len(carriers)
                carriers.append(at)
                if engine is nc.vector:
                    engine.memset(carried[:, at:at + 1], 0.0)
                else:
                    engine.tensor_tensor(carried[:, at:at + 1], nhalf[:, 0:1], nhalf[:, 0:1], ALU.add)

        def tok_dram(a, b):
            return a[b, :, :].rearrange("(t p) c -> p t c", p=P)

        def tok_bank(tile, i):
            return tile[:, i * TB:(i + 1) * TB, :]

        def bank3(bank):
            return bank.rearrange("p (t c) -> p t c", t=TB)

        def steps(eng, first_step, second_step, step, last_steps):
            first_step()
            second_step()
            with eng.Fori(LAG, B - 1, 2) as j:
                for q in range(2):
                    step(j + q, q)
            last_steps(B - 1, B - 2)

        block = ctx.enter_context(nc.Block())

        @block.sync
        def _(sp):
            sp.sem_inc(stored, 16)
            sp.dma_start(ids_row[:, :], ids.rearrange("(a k) -> a k", a=1)).then_inc(s_ids, 16)
            sp.dma_start(x1[0][:, :, :], tok_dram(x, 0)).then_inc(x_loaded, 16)
            load_adapters(sp, range(0, K, 2))

            def load_weights(group):
                for n, dst, src in group:
                    sp.dma_start(dst, src.rearrange("(h p) o -> p h o", p=P)).then_inc(s_wload[n], 16)

            load_weights((("wk", wk_raw, wk), ("wv", wv_raw, wv)))

            def load(j, q):
                if isinstance(j, int) and (j == 0 or j >= B):
                    return
                if has(j - 2):
                    sp.wait_ge(xs_done, j - 1)
                sp.wait_ge(x_loaded, 16 * (j - 1) + 16)
                sp.dma_start(x1[q][:, :, :], tok_dram(x, j)).then_inc(x_loaded, 16)

            def store(b, q):
                if has(b):
                    sp.wait_ge(stored, 16 * b + 16)
                    sp.wait_ge(x3_done, 2 * b + 2 + SEED)
                    sp.dma_start(tok_dram(out, b), xs[q][:, :, :]).then_inc(stored, 16)

            first, end = 3, 7
            for j in range(first):
                load(j, j % 2)
                if j == 1:
                    load_weights((("wr", wr_sb[:, :, :], wr), ("wcr", wcr_raw, wcr), ("wo", wo_sb[:, :, :], wo), ("wck", wck_raw, wck)))
                    for i, src in enumerate(wcv.rearrange("(i h p) o -> i p h o", i=2, p=P)[i] for i in range(2)):
                        sp.dma_start(wcv_raw[i], src).then_inc(s_wload["wcv"], 16)
            with sp.Fori(first, end - 1, 2) as j:
                for i in range(2):
                    load(j + i, (first + i) % 2)
                    store(j + i - 3, (first + i - 3) % 2)
            for j in range(end, B + 2):
                load(j, j % 2)
                store(j - 3, (j - 3) % 2)
            for i in range(BANKS):
                sp.wait_ge(x3_done, 2 * (B - 1) + i + 1 + SEED)
                sp.dma_start(tok_bank(tok_dram(out, B - 1), i), tok_bank(xs[(B - 1) % 2], i)).then_inc(stored, 16)
            sp.wait_ge(stored, 16 * (B + 2))

        @block.tensor
        def _(pe):
            def product32(bank, stationary, moving, first, last):
                return nc.tensor.matmul(bank, stationary, moving, start=first, stop=last)

            def product_split(bank, stationary, moving, first, last):
                (sh, sl), (mh, ml) = stationary, moving
                nc.tensor.matmul(bank, sh, mh, start=first, stop=False)
                nc.tensor.matmul(bank, sh, ml, start=False, stop=False)
                return nc.tensor.matmul(bank, sl, mh, start=False, stop=last)

            def turn(stage, kind, tile, b):
                for h in range(CH):
                    take_bank(pe, stage, h, b)
                    if h == 0:
                        pe.wait_ge(normed[kind], b + 1)
                    for t in range(NT):
                        last = nc.tensor.transpose(bank_of(stage, h)[:, t * P:(t + 1) * P], tile[:, t, h * P:(h + 1) * P], ident[:, :])
                    last.then_inc(turned[kind], 1)

            def to_tokens(stage, src, w, done, b, banks=range(BANKS), split=False):
                for i in banks:
                    take_bank(pe, stage, i, b)
                    for t in range(TB):
                        tok = (i * TB + t) * P
                        for h in range(CH):
                            out_part, first, end = bank_of(stage, i)[:, t * C:(t + 1) * C], h == 0, h == CH - 1
                            if split:
                                last = product_split(out_part, [part[:, h, tok:tok + P] for part in src], [part[:, h, :] for part in w],
                                                     first, end)
                            else:
                                last = product32(out_part, src[:, h, tok:tok + P], w[:, h, :], first, end)
                    last.then_inc(done, 1)

            def to_channels(bank, src, w, o):
                for h in range(CH):
                    last = product32(bank, w[:, h, o * P:(o + 1) * P], src[:, h, :], h == 0, h == CH - 1)
                return last

            def to_channels_split(bank, src, w, o):
                for h in range(CH):
                    last = product_split(bank, [part[:, h, o * P:(o + 1) * P] for part in w], [part[:, h, :] for part in src],
                                         h == 0, h == CH - 1)
                return last

            pe.wait_ge(s_const, 3)

            def ffn_bias():
                pe.wait_ge(s_gate_rows, 1)
                pe.wait_ge(s_bias_sel, 16 * K)
                nc.tensor.matmul(k_ps[:, 0, 0:C], gate_rows[:, :], bias_sel[:, :], start=True, stop=True).then_inc(s_bias_ps, 1)

            def front_k(f):
                if isinstance(f, int) and f == 0:
                    pe.wait_ge(s_small_hi, 1)
                    pe.wait_ge(s_small_lo, 1)
                    pe.wait_ge(s_bias, 1)
                pe.wait_ge(xk_hi_done, 2 * f + 2)
                pe.wait_ge(xk_lo_done, 2 * f + 2)
                for o in range(CH):
                    reused(pe, z_done, 2 * (f - 1) + o + 1, f)
                    to_channels_split(k_ps[:, o, :], (xk_hi, xk_lo), (wk_hi, wk_lo), o).then_inc(kp_ps, 1)

            def front_v(f, o):
                if isinstance(f, int) and f == 0:
                    pe.wait_ge(s_small_hi, 2)
                    pe.wait_ge(s_small_lo, 2)
                pe.wait_ge(xv_hi_done, 2 * f + 2)
                pe.wait_ge(xv_lo_done, 2 * f + 2)
                reused(pe, t1_done, 2 * (f - 1) + o + 1, f)
                to_channels_split(v_ps[:, o, :], (xv_hi, xv_lo), (wv_hi, wv_lo), o).then_inc(vp_ps, 1)

            def front_r(f):
                if isinstance(f, int) and f == 0:
                    pe.wait_ge(s_wload["wr"], 16)
                pe.wait_ge(xr_done, 2 * f + 2)
                for o in range(CH):
                    take_bank(pe, "r", o, f)
                    to_channels(bank_of("r", o), dr, wr_sb, o).then_inc(r_ps, 1)

            def channel_keys(e):
                if isinstance(e, int) and e == 0 or not isinstance(e, int):
                    pe.wait_ge(s_wck_hi, 1)
                    pe.wait_ge(s_wlo, 1)
                pe.wait_ge(xck_hi_done, 2 * e + 2)
                pe.wait_ge(xck_lo_done, 2 * e + 2)
                for n in range(HB):
                    stage, i = f"kk{n // 2 * 2}", n % 2
                    take_bank(pe, stage, i, e)
                    for h in range(CH):
                        last = product_split(bank_of(stage, i), (wck_hi[:, h, n * P:(n + 1) * P], wck_lo[:, h, n * P:(n + 1) * P]),
                                             (xck_hi[:, h, :], xck_lo[:, h, :]), h == 0, h == CH - 1)
                    last.then_inc(kk_ps, 1)

            def channel_values(e, t):
                i, tok = t // TB, t * P
                if t == 0:
                    pe.wait_ge(s_wcv_hi, 2)
                    pe.wait_ge(s_wlo, 3)
                if t % TB == 0:
                    take_bank(pe, "kv", i, e)
                for n in range(HB):
                    if t == 0:
                        pe.wait_ge(*high_done(e, n))
                        pe.wait_ge(*rest_done(e, n))
                    last = product_split(bank_of("kv", i)[:, t % TB * C:(t % TB + 1) * C],
                                         (kk_hi[:, n, tok:tok + P], kk_lo[:, n, tok:tok + P]),
                                         (wcv_hi[:, n, :], wcv_lo[:, n, :]), n == 0, n == HB - 1)
                if t % TB == TB - 1:
                    last.then_inc(kv_ps, 1)

            def first_product(f):
                pe.wait_ge(ffn1_in, 2 * f + 2)
                to_tokens("y1", ffn_in, ffn_t, y1_ps, f)

            def second_product(e):
                pe.wait_ge(ffn2_in, 2 * e + 2)
                to_tokens("y2", ffn_in, ffn_t, y2_ps, e)

            def output_product(m):
                pe.wait_ge(rwkv_done, 2 * m + 2)
                to_tokens("o", rwkv, wo_sb, o_ps, m)

            def channel_gate(e):
                pe.wait_ge(xcr_hi_done, 2 * e + 2)
                pe.wait_ge(xcr_lo_done, 2 * e + 2)
                to_tokens("cr", (xcr_hi, xcr_lo), (wcr_hi, wcr_lo), cr_ps, e, split=True)

            def turn_x2(e):
                pe.wait_ge(normed_act, e + 1)
                turn("turn_x2", "x2", norm, e)

            def first_step():
                turn("turn_x", "x", norm, 0)
                ffn_bias()
                pe.wait_ge(s_ffn_acc, K)
                first_product(0)
                turn("turn_x", "x", norm, 1)
                turn("turn_x1", "x1", norm, 0)
                first_product(1)
                front_k(0)
                front_v(0, 0)
                front_v(0, 1)
                front_r(0)

            def second_step():
                turn("turn_x1", "x1", norm, 1)
                pe.wait_ge(s_wo, 1)
                output_product(0)
                front_k(1)
                front_v(1, 0)
                front_v(1, 1)
                turn("turn_xa", "xa", norm, 0)
                front_r(1)

            def step(j, q):
                f, m, e = j, j - 1, j - 2
                pe.wait_ge(s_small_hi, 3)
                pe.wait_ge(s_small_lo, 3)
                channel_keys(e)
                turn("turn_x", "x", norm, f)
                channel_values(e, 0)
                channel_values(e, 1)
                first_product(f)
                output_product(m)
                channel_gate(e)
                turn("turn_x1", "x1", norm, f)
                channel_values(e, 2)
                channel_values(e, 3)
                turn("turn_xa", "xa", norm, m)
                front_k(f)
                front_v(f, 0)
                front_v(f, 1)
                turn_x2(e)
                second_product(e)
                front_r(f)

            def last_steps(m, e):
                channel_keys(e)
                channel_gate(e)
                channel_values(e, 0)
                channel_values(e, 1)
                channel_values(e, 2)
                output_product(m)
                channel_values(e, 3)
                turn("turn_xa", "xa", norm, m)
                turn_x2(e)
                second_product(e)
                channel_keys(m)
                channel_gate(m)
                for t in range(NT):
                    channel_values(m, t)
                for i in range(BANKS):
                    pe.wait_ge(*taken[True, i])
                    pe.wait_ge(last_normed_pool, i + 1)
                    pe.wait_ge(last_normed_act, i + 1)
                    for h in range(CH):
                        for t in range(TB):
                            last = nc.tensor.transpose(last_bank(i)[:, h, t * P:(t + 1) * P],
                                                       norm[:, i * TB + t, h * P:(h + 1) * P], ident[:, :])
                    last.then_inc(last_turned, 1)
                    pe.wait_ge(last_in, i + 1)
                    to_tokens("y2", ffn_in, ffn_t, y2_ps, m, (i,))

            steps(pe, first_step, second_step, step, last_steps)

        @block.scalar
        def _(act):
            act.dma_start(gate_col[:, :], gates.rearrange("(k a) -> k a", a=1)).then_inc(s_small, 16)
            act.dma_start(gates_bc[:, :], gates.rearrange("(a k) -> a k", a=1).broadcast_to([P, K])).then_inc(s_gates, 16)
            act.dma_start(vec[:, :, :], vectors).then_inc(s_vec, 16)
            load_adapters(act, range(1, K, 2))
            act.wait_ge(s_vec, 16)
            nc.scalar.activation(decay[:, :], V["time_decay"], ACT.Exp).then_inc(s_decay, 1)

            def evac(kind, dst, done, b):
                for h in range(CH):
                    act.wait_ge(turned[kind], 2 * b + h + 1)
                    nc.scalar.activation(dst[:, h, :], bank_of(f"turn_{kind}", h), ACT.Copy).then_inc(done, 1)

            def evac_affine(kind, dst, done, g, off, b):
                for h in range(CH):
                    act.wait_ge(turned[kind], 2 * b + h + 1)
                    nc.scalar.activation(dst[:, h, 1:PAD], bank_of(f"turn_{kind}", h), ACT.Identity,
                                         scale=V[g][:, h:h + 1], bias=V[off][:, h:h + 1]).then_inc(done, 1)

            def key_relu(b, n):
                if n >= KK_BUFS:
                    act.wait_ge(*rest_done(b, n - KK_BUFS))
                act.wait_ge(kk_ps, HB * b + n + 1)
                nc.scalar.activation(kk[:, n % KK_BUFS, :], bank_of(f"kk{n // 2 * 2}", n % 2), ACT.Relu).then_inc(relu_done, 1)

            def key_square(b, n):
                act.wait_ge(relu_done, HB * b + n + 1)
                nc.scalar.activation(kk[:, n % KK_BUFS, :], kk[:, n % KK_BUFS, :], ACT.Square).then_inc(sq_done, 1)

            def key_high(b, n):
                act.wait_ge(sq_done, HB * b + n + 1)
                nc.scalar.activation(kk_hi[:, n, :], kk[:, n % KK_BUFS, :], ACT.Copy).then_inc(high_act, 1)

            def rectify(m, h, src, ready, pos, neg, done):
                act.wait_ge(ready, 2 * m + h + 1)
                nc.scalar.activation(pos[:, h, 0:T], src[:, h, 0:T], ACT.Relu)
                nc.scalar.activation(neg[:, h, 0:T], src[:, h, 0:T], ACT.Relu, scale=-1.0).then_inc(done, 1)

            def exponentials(m, h, pos, neg, ready, done):
                act.wait_ge(ready, 2 * m + h + 1)
                nc.scalar.activation(pos[:, h, 0:T], pos[:, h, 0:T], ACT.Exp, scale=-1.0)
                nc.scalar.activation(neg[:, h, 0:T], neg[:, h, 0:T], ACT.Exp, scale=-1.0).then_inc(done, 1)

            def scaled_share(e, q):
                act.wait_ge(shift_done, e + 1)
                for t in range(TB, NT):
                    last = nc.scalar.activation(norm[:, t, :], xs[q][:, t, :], ACT.Identity, scale=rstd["x2"][:, t:t + 1],
                                                bias=shift_x2[:, t:t + 1])
                last.then_inc(normed_act, 1)

            def small_weight_highs():
                for n, raw, hi in (("wk", wk_raw, wk_hi), ("wv", wv_raw, wv_hi), ("wcr", wcr_raw, wcr_hi)):
                    act.wait_ge(s_wload[n], 16)
                    nc.scalar.activation(hi[:, :, :], raw, ACT.Copy).then_inc(s_small_hi, 1)

            def split_weights():
                act.wait_ge(s_wload["wo"], 16)
                nc.scalar.activation(wo_sb[:, :, :], wo_sb[:, :, :], ACT.Copy, scale=0.5).then_inc(s_wo, 1)
                act.wait_ge(s_wload["wck"], 16)
                nc.scalar.activation(wck_hi[:, :, :], wck_raw, ACT.Copy).then_inc(s_wck_hi, 1)
                act.wait_ge(s_wload["wcv"], 32)
                for i in range(2):
                    nc.scalar.activation(wcv_raw[i], wcv_raw[i], ACT.Copy, scale=0.5).then_inc(s_wcv_half, 1)
                for i in range(2):
                    act.wait_ge(s_wcv_half, i + 1)
                    nc.scalar.activation(wcv_hi[:, i * NT:(i + 1) * NT, :], wcv_raw[i], ACT.Copy).then_inc(s_wcv_hi, 1)

            def keys(e):
                key_relu(e, 0)
                for n in range(HB):
                    if n + 1 < HB:
                        key_relu(e, n + 1)
                    key_square(e, n)
                    if n in ACT_HIGHS:
                        key_high(e, n)

            def rough_reciprocal(m):
                act.preload_act_table_set("natural_log_exp_and_others")
                for h in range(CH):
                    act.wait_ge(den_done, 2 * m + h + 1)
                    nc.scalar.activation(eb_v[:, h, 0:T], e_v[:, h, 0:T], ACT.Ln).then_inc(ln_done, 1)
                for h in range(CH):
                    act.wait_ge(ln_done, 2 * m + h + 1)
                    nc.scalar.activation(eb_v[:, h, 0:T], eb_v[:, h, 0:T], ACT.Exp, scale=-1.0).then_inc(r0_done, 1)

            def channel_gate(e):
                for i in range(BANKS):
                    act.wait_ge(cr_ps, 2 * e + i + 1)
                    nc.scalar.activation(tok_bank(thc, i), bank3(bank_of("cr", i)), ACT.Tanh, scale=0.5).then_inc(thc_done, 1)

            def high_part(dst, src, ready, done, b):
                for h in range(CH):
                    act.wait_ge(ready, 2 * b + h + 1)
                    nc.scalar.activation(dst[:, h, :], src[:, h, :], ACT.Copy).then_inc(done, 1)

            def front_highs(f):
                high_part(xk_hi, xk, xk_done, xk_hi_done, f)
                high_part(xv_hi, xv, xv_done, xv_hi_done, f)

            def key_input_high(m):
                if not (isinstance(m, int) and m == B - 1):
                    act.wait_ge(kp_ps, 2 * (m + 1) + 2)
                for h in range(CH):
                    act.wait_ge(xck_done, 2 * m + h + 1)
                    nc.scalar.activation(xck_hi[:, h, :], xck[:, h, :], ACT.Copy).then_inc(xck_hi_done, 1)

            def state_exponentials(f):
                for h in range(CH):
                    rectify(f, h, z2, z2_done, eb_v, eb_s, rect2)
                for h in range(CH):
                    exponentials(f, h, eb_v, eb_s, rect2, eb_done)

            def output_rectify(f):
                for h in range(CH):
                    rectify(f, h, z, z_done, e_s, e_v, rect)

            def time_gate(f, h):
                act.wait_ge(r_ps, 2 * f + h + 1)
                nc.scalar.activation(thr[:, h, :], bank_of("r", h), ACT.Tanh, scale=0.5).then_inc(thr_done, 1)

            def output_exponentials(f):
                output_rectify(f)
                for h in range(CH):
                    time_gate(f, h)
                    exponentials(f, h, e_s, e_v, rect, e_done)

            def h1_of(f):
                evac_affine("x1", h1, h1_done, "ln1_g", "ln1_b", f)

            def h2_of(m):
                evac_affine("xa", h2, h2_done, "ln2_g", "ln2_b", m)

            def first_step():
                evac("x", ffn_in, ffn1_in, 0)
                small_weight_highs()
                evac("x", ffn_in, ffn1_in, 1)
                split_weights()
                h1_of(0)
                front_highs(0)
                for h in range(CH):
                    exponentials(0, h, eb_v, eb_s, rect2, eb_done)
                for h in range(CH):
                    exponentials(0, h, e_s, e_v, rect, e_done)
                for h in range(CH):
                    time_gate(0, h)

            def second_step():
                h1_of(1)
                rough_reciprocal(0)
                front_highs(1)
                h2_of(0)
                key_input_high(0)
                for h in range(CH):
                    time_gate(1, h)
                for h in range(CH):
                    exponentials(1, h, eb_v, eb_s, rect2, eb_done)
                for h in range(CH):
                    exponentials(1, h, e_s, e_v, rect, e_done)

            def step(j, q):
                f, m, e = j, j - 1, j - 2
                keys(e)
                rough_reciprocal(m)
                evac("x", ffn_in, ffn1_in, f)
                channel_gate(e)
                h1_of(f)
                front_highs(f)
                h2_of(m)
                scaled_share(e, q)
                key_input_high(m)
                evac("x2", ffn_in, ffn2_in, e)
                state_exponentials(f)
                output_exponentials(f)

            def last_steps(m, e):
                keys(e)
                channel_gate(e)
                rough_reciprocal(m)
                h2_of(m)
                scaled_share(e, e % 2)
                key_input_high(m)
                evac("x2", ffn_in, ffn2_in, e)
                keys(m)
                channel_gate(m)
                for i in range(BANKS):
                    t = i * TB + 1
                    act.wait_ge(last_shift, i + 1)
                    nc.scalar.activation(norm[:, t, :], xs[m % 2][:, t, :], ACT.Identity, scale=rstd["x2"][:, t:t + 1],
                                         bias=shift_x2[:, t:t + 1]).then_inc(last_normed_act, 1)
                    act.wait_ge(last_turned, i + 1)
                    nc.scalar.activation(ffn_in[:, :, i * TB * P:(i + 1) * TB * P], last_bank(i), ACT.Copy).then_inc(last_in, 1)

            steps(act, first_step, second_step, step, last_steps)

        @block.vector
        def _(dve):
            dve.sem_inc(x3_done, SEED)
            dve.wait_ge(s_gates, 16)
            nc.vector.tensor_scalar(gates_bc[:, :], gates_bc[:, :], 0.5, None, ALU.mult).then_inc(s_gates, 1)

            def tile_stats(kind, tile, tiles):
                for t in tiles:
                    last = nc.vector.bn_stats(bn[kind][:, t, :], tile[:, t, :])
                return last

            def aggregate(kind, b):
                dve.wait_ge(bn_done[kind], b + 1)
                own_wait(nc.vector, b)
                for t in range(NT):
                    last = nc.vector.bn_aggr(mv[kind][:, t, :], bn[kind][:, t, :])
                last.then_inc(mv_done[kind], 1)

            def stats_of_bank(kind, tile, b, i, ready):
                dve.wait_ge(ready, 2 * b + i + 1)
                last = tile_stats(kind, tile, range(i * TB, (i + 1) * TB))
                if i == BANKS - 1:
                    last.then_inc(bn_done[kind], 1)
                    aggregate(kind, b)

            def stats(kind, tile, b):
                tile_stats(kind, tile, range(NT)).then_inc(bn_done[kind], 1)
                aggregate(kind, b)

            def ffn_weights():
                dve.wait_ge(s_gates, 17)
                for k in range(K):
                    if k == K - 1:
                        dve.wait_ge(s_decay, 1)
                        nc.vector.tensor_scalar(decay[:, :], decay[:, :], -1.0, None, ALU.mult).then_inc(s_decay_neg, 1)
                        dve.wait_ge(s_small, 16)
                        dve.wait_ge(s_const, 2)
                        nc.vector.tensor_scalar(gate_rows[:, :], gate_rows[:, :], gate_col[:, 0:1], 0.5, ALU.mult, ALU.mult).then_inc(s_gate_rows, 1)
                    dve.wait_ge(s_sel[k], 16)
                    g = gates_bc[:, k:k + 1]
                    if k == 0:
                        nc.vector.tensor_scalar(ffn_t[:, :, :], sel[:, 0, :, :], g, None, ALU.mult).then_inc(s_ffn_acc, 1)
                    else:
                        dve.wait_ge(s_ffn_acc, k)
                        nc.vector.scalar_tensor_tensor(ffn_t[:, :, :], sel[:, k, :, :], g, ffn_t[:, :, :], ALU.mult, ALU.add).then_inc(s_ffn_acc, 1)
                dve.wait_ge(s_ffn_acc, K)
                nc.vector.memset(pp[:, :, 0:1], NEG)
                nc.vector.memset(aa[:, :, 0:1], 0.0)
                nc.vector.memset(bb[:, :, 0:1], 0.0).then_inc(s_pads, 1)
                dve.wait_ge(s_bias_ps, 1)
                nc.vector.tensor_copy(bias_bc[:, :], k_ps[:, 0, 0:C]).then_inc(s_bias, 1)

            def small_weight_rest(i, raw, hi, lo):
                dve.wait_ge(s_small_hi, i + 1)
                nc.vector.tensor_tensor(lo[:, :, :], raw, hi[:, :, :].bitcast(F32), ALU.subtract).then_inc(s_small_lo, 1)

            def weight_rests():
                dve.wait_ge(s_wck_hi, 1)
                nc.vector.tensor_tensor(wck_lo[:, :, :], wck_raw, wck_hi[:, :, :].bitcast(F32), ALU.subtract).then_inc(s_wlo, 1)
                for i in range(2):
                    dve.wait_ge(s_wcv_hi, i + 1)
                    nc.vector.tensor_tensor(wcv_lo[:, i * NT:(i + 1) * NT, :], wcv_raw[i], wcv_hi[:, i * NT:(i + 1) * NT, :].bitcast(F32),
                                            ALU.subtract).then_inc(s_wlo, 1)

            def wkv_exponents(m):
                dve.wait_ge(xk_lo_done, 2 * m + 2)
                dve.wait_ge(xv_lo_done, 2 * m + 2)
                for h in range(CH):
                    dve.wait_ge(kp_ps, 2 * m + h + 1)
                    nc.vector.tensor_tensor_scan(pp[:, h, 1:PAD], decay[:, h:h + 1].to_broadcast([P, T]), k_ps[:, h, :],
                                                 NEG, ALU.add, ALU.max).then_inc(pp_done, 1)
                for h in range(CH):
                    dve.wait_ge(pp_done, 2 * m + h + 1)
                    nc.vector.scalar_tensor_tensor(z2[:, h, 0:T], pp[:, h, 0:T], decay[:, h:h + 1], k_ps[:, h, :],
                                                   ALU.add, ALU.subtract).then_inc(z2_done, 1)
                for h in range(CH):
                    nc.vector.scalar_tensor_tensor(z[:, h, 0:T], k_ps[:, h, :], V["time_first"][:, h:h + 1], pp[:, h, 0:T],
                                                   ALU.add, ALU.subtract).then_inc(z_done, 1)

            def rectify(m, src, ready, pos, neg, done):
                for h in range(CH):
                    dve.wait_ge(ready, 2 * m + h + 1)
                    nc.vector.tensor_scalar(pos[:, h, 0:T], src[:, h, 0:T], 0.0, None, ALU.max)
                    nc.vector.tensor_scalar(neg[:, h, 0:T], src[:, h, 0:T], -1.0, 0.0, ALU.mult, ALU.max).then_inc(done, 1)

            def wkv_terms(m):
                for h in range(CH):
                    dve.wait_ge(e_done, 2 * m + h + 1)
                    nc.vector.tensor_tensor(z[:, h, 0:T], e_v[:, h, 0:T], v_ps[:, h, :], ALU.mult).then_inc(t1_done, 1)

            def wkv_states(m):
                for h in range(CH):
                    dve.wait_ge(eb_done, 2 * m + h + 1)
                    nc.vector.tensor_tensor_scan(bb[:, h, 1:PAD], eb_s[:, h, 0:T], eb_v[:, h, 0:T], 0.0, ALU.mult, ALU.add).then_inc(bb_done, 1)
                    dve.wait_ge(vp_ps, 2 * m + h + 1)
                    nc.vector.tensor_tensor(z2[:, h, 0:T], eb_v[:, h, 0:T], v_ps[:, h, :], ALU.mult).then_inc(ev_done, 1)
                for h in range(CH):
                    dve.wait_ge(ev_done, 2 * m + h + 1)
                    nc.vector.tensor_tensor_scan(aa[:, h, 1:PAD], eb_s[:, h, 0:T], z2[:, h, 0:T], 0.0, ALU.mult, ALU.add).then_inc(aa_done, 1)

            def wkv_denominator(m):
                for h in range(CH):
                    dve.wait_ge(t3_done, 2 * m + h + 1)
                    nc.vector.tensor_tensor(e_v[:, h, 0:T], e_v[:, h, 0:T], eb_v[:, h, 0:T], ALU.add).then_inc(den_done, 1)

            def wkv_numerator(m):
                for h in range(CH):
                    dve.wait_ge(t2_done, 2 * m + h + 1)
                    dve.wait_ge(t1_done, 2 * m + h + 1)
                    nc.vector.tensor_tensor(z[:, h, 0:T], z[:, h, 0:T], z2[:, h, 0:T], ALU.add).then_inc(num_done, 1)

            def wkv_reciprocal(m):
                dve.wait_ge(r0_done, 2 * m + 2)
                nc.vector.tensor_tensor(eb_s[:, 1, 0:T], e_v[:, 1, 0:T], eb_v[:, 1, 0:T], ALU.mult).then_inc(dr0_dve, 1)
                for h in range(CH):
                    dve.wait_ge((dr0_pool, dr0_dve)[h], m + 1)
                    nc.vector.scalar_tensor_tensor(eb_s[:, h, 0:T], eb_s[:, h, 0:T], 2.0, eb_v[:, h, 0:T], ALU.subtract, ALU.mult,
                                                   reverse0=True).then_inc(rec_done, 1)

            def wkv_gate(m):
                for h in range(CH):
                    dve.wait_ge(num_done, 2 * m + h + 1)
                    dve.wait_ge(thr_done, 2 * m + h + 1)
                    nc.vector.scalar_tensor_tensor(z[:, h, 0:T], thr[:, h, :], 1.0, z[:, h, 0:T], ALU.add, ALU.mult).then_inc(gated_done, 1)

            def wkv_quotient(m):
                for h in range(CH):
                    dve.wait_ge(rec_done, 2 * m + h + 1)
                    dve.wait_ge(gated_done, 2 * m + h + 1)
                    nc.vector.tensor_tensor(rwkv[:, h, :], z[:, h, 0:T], eb_s[:, h, 0:T], ALU.mult).then_inc(rwkv_done, 1)

            def key_high(e, n):
                dve.wait_ge(sq_done, HB * e + n + 1)
                nc.vector.tensor_copy(kk_hi[:, n, :], kk[:, n % KK_BUFS, :]).then_inc(high_dve, 1)

            def value_sum(e, i, q):
                dve.wait_ge(kv_ps, 2 * e + i + 1)
                dve.wait_ge(thc_done, 2 * e + i + 1)
                nc.vector.scalar_tensor_tensor(tok_bank(thc, i), tok_bank(thc, i), 1.0, bank3(bank_of("kv", i)), ALU.add, ALU.mult).then_inc(kvs_done, 1)
                dve.wait_ge(kvs_done, 2 * e + i + 1)
                dve.wait_ge(xs_done, e + 1)
                nc.vector.tensor_tensor(tok_bank(xs[q], i), tok_bank(xs[q], i), tok_bank(thc, i), ALU.add).then_inc(x2_done, 1)

            def mix(dst, d, h, prev, m, done):
                for c in range(CH):
                    nc.vector.scalar_tensor_tensor(dst[:, c, :], d[:, c, :], V[m][:, c:c + 1], h[:, c, prev:prev + T],
                                                   ALU.mult, ALU.add).then_inc(done, 1)

            def difference(dst, h, ready, b, done):
                for c in range(CH):
                    dve.wait_ge(ready, 2 * b + c + 1)
                    nc.vector.tensor_tensor(dst[:, c, :], h[:, c, 1:PAD], h[:, c, 0:T], ALU.subtract).then_inc(done, 1)
                dve.wait_ge(done, 2 * b + 2)

            def stats_x(f, q):
                dve.wait_ge(x_loaded, 16 * f + 16)
                stats("x", x1[q], f)

            def add_first(f, q):
                if not isinstance(f, int):
                    dve.wait_ge(rs1_steps, 2 * f)
                for i in range(BANKS):
                    dve.wait_ge(y1_ps, 2 * f + i + 1)
                    dve.wait_ge(xb_done, f + 1)
                    nc.vector.tensor_tensor(tok_bank(x1[q], i), tok_bank(x1[q], i), bank3(bank_of("y1", i)), ALU.add).then_inc(x1_done, 1)
                dve.wait_ge(x1_done, 2 * f + 2)
                stats("x1", x1[q], f)

            def add_output(m):
                for i in range(BANKS):
                    dve.wait_ge(o_ps, 2 * m + i + 1)
                    dve.wait_ge(xa_done, m + 1)
                    nc.vector.tensor_tensor(tok_bank(xa, i), tok_bank(xa, i), bank3(bank_of("o", i)), ALU.add).then_inc(xa2_done, 1)
                    stats_of_bank("xa", xa, m, i, xa2_done)

            def add_values(e, i, q):
                value_sum(e, i, q)
                stats_of_bank("x2", xs[q], e, i, x2_done)

            def add_second_bank(i, q):
                nc.vector.tensor_tensor(tok_bank(xs[q], i), tok_bank(xs[q], i), bank3(bank_of("y2", i)), ALU.add).then_inc(x3_done, 1)

            def add_second(e, q):
                for i in range(BANKS):
                    dve.wait_ge(y2_ps, 2 * e + i + 1)
                    dve.wait_ge(x2b_done, e + 1)
                    add_second_bank(i, q)

            def mix_k(f):
                difference(dr, h1, h1_done, f, d1_done)
                mix(xk, dr, h1, 0, "tm_k", xk_done)

            def mix_v(f):
                mix(xv, dr, h1, 0, "tm_v", xv_done)

            def mix_r(f):
                mix(dr, dr, h1, 0, "tm_r", xr_done)

            def mix_ck(m):
                difference(dcr, h2, h2_done, m, d2_done)
                mix(xck, dcr, h2, 0, "cm_k", xck_done)

            def mix_cr(m):
                mix(dcr, dcr, h2, 0, "cm_r", xcr_done)
                if not (isinstance(m, int) and m == B - 1):
                    dve.wait_ge(vp_ps, 2 * (m + 1) + 2)
                for h in range(CH):
                    dve.wait_ge(xcr_done, 2 * m + h + 1)
                    nc.vector.tensor_copy(xcr_hi[:, h, :], dcr[:, h, :]).then_inc(xcr_hi_done, 1)

            def wkv_end(m):
                wkv_numerator(m)
                wkv_gate(m)
                wkv_reciprocal(m)
                wkv_quotient(m)

            def keys(e, between):
                key_rest(nc.vector, dve, e, 0)
                key_high(e, 1)
                key_rest(nc.vector, dve, e, 1)
                key_high(e, 2)
                key_rest(nc.vector, dve, e, 2)
                key_high(e, 3)
                between()
                key_high(e, 4)
                key_rest(nc.vector, dve, e, 4)
                key_high(e, 5)
                key_high(e, 6)
                key_rest(nc.vector, dve, e, 6)
                key_high(e, 7)
                key_rest(nc.vector, dve, e, 7)

            def first_step():
                stats_x(0, 0)
                ffn_weights()
                dve.wait_ge(normed["x"], 1)
                stats_x(1, 1)
                small_weight_rest(0, wk_raw, wk_hi, wk_lo)
                small_weight_rest(1, wv_raw, wv_hi, wv_lo)
                add_first(0, 0)
                small_weight_rest(2, wcr_raw, wcr_hi, wcr_lo)
                weight_rests()
                mix_k(0)
                mix_v(0)
                mix_r(0)
                dve.wait_ge(rs1_steps, 2)
                add_first(1, 1)
                dve.wait_ge(s_pads, 1)
                wkv_exponents(0)
                rectify(0, z2, z2_done, eb_v, eb_s, rect2)
                rectify(0, z, z_done, e_s, e_v, rect)

            def second_step():
                wkv_states(0)
                wkv_terms(0)
                wkv_denominator(0)
                wkv_end(0)
                mix_k(1)
                mix_v(1)
                mix_r(1)
                add_output(0)
                wkv_exponents(1)
                mix_ck(0)
                rectify(1, z2, z2_done, eb_v, eb_s, rect2)
                key_input_rest(nc.vector, dve, 0)
                rectify(1, z, z_done, e_s, e_v, rect)
                mix_cr(0)

            def step(j, q):
                f, m, e = j, j - 1, j - 2
                stats_x(f, q)
                wkv_states(m)
                wkv_terms(m)
                keys(e, lambda: wkv_denominator(m))
                wkv_end(m)
                add_first(f, q)
                add_output(m)
                add_values(e, 0, q)
                mix_k(f)
                mix_v(f)
                add_values(e, 1, q)
                mix_ck(m)
                wkv_exponents(f)
                mix_r(f)
                mix_cr(m)
                add_second(e, q)

            def last_steps(m, e):
                wkv_states(m)
                wkv_terms(m)
                keys(e, lambda: wkv_denominator(m))
                wkv_end(m)
                add_values(e, 0, e % 2)
                add_output(m)
                add_values(e, 1, e % 2)
                mix_ck(m)
                mix_cr(m)
                key_input_rest(nc.vector, dve, m)
                gate_input_rest(nc.vector, dve, m)
                add_second(e, e % 2)
                keys(m, lambda: None)
                for i in range(BANKS):
                    value_sum(m, i, m % 2)
                    dve.wait_ge(x2_done, 2 * m + i + 1)
                    tiles = range(i * TB, (i + 1) * TB)
                    tile_stats("x2", xs[m % 2], tiles).then_inc(bn_done["x2"], 1)
                    dve.wait_ge(bn_done["x2"], m + i + 1)
                    for t in tiles:
                        last = nc.vector.bn_aggr(mv["x2"][:, t, :], bn["x2"][:, t, :])
                    last.then_inc(last_mv, 1)
                for i in range(BANKS):
                    dve.wait_ge(y2_ps, 2 * m + i + 1)
                    dve.wait_ge(last_bias, i + 1)
                    add_second_bank(i, m % 2)

            steps(dve, first_step, second_step, step, last_steps)

        @block.gpsimd
        def _(pool):
            nc.gpsimd.memset(ident[:, :], 0.0).then_inc(s_const, 1)
            nc.gpsimd.memset(gate_rows[:, :], 1.0).then_inc(s_const, 1)
            pool.wait_ge(s_const, 1)
            nc.gpsimd.affine_select(out=ident[:, :], in_=ident[:, :], compare_op=ALU.not_equal, fill=1.0, base=0,
                                    pattern=[[-1, P]], channel_multiplier=1).then_inc(s_const, 1)
            nc.gpsimd.memset(nhalf[:, :], -0.5)
            nc.gpsimd.memset(minus[:, :], -1.0)
            nc.gpsimd.memset(eps[:, :], EPS)
            nc.gpsimd.memset(eps_sq[:, :], EPS * EPS)
            nc.gpsimd.memset(one_eps[:, :], 1.0 + EPS)
            nc.gpsimd.memset(h1[:, :, 0:1], 0.0)
            nc.gpsimd.memset(h2[:, :, 0:1], 0.0).then_inc(s_const, 1)
            pool.wait_ge(s_const, 4)

            def inverse_std(kind, b):
                pool.wait_ge(mv_done[kind], b + 1)
                nc.gpsimd.tensor_tensor(vare[kind][:, :], mv[kind][:, :, 1], eps[:, :], ALU.add).then_inc(rs_steps[kind], 1)
                nc.gpsimd.tensor_tensor(negm[kind][:, :], mv[kind][:, :, 0], minus[:, :], ALU.mult).then_inc(rs_steps[kind], 1)
                pool.wait_ge(rs_steps[kind], 3 * b + 1)
                nc.gpsimd.tensor_tensor(rstd[kind][:, :], vare[kind][:, :], nhalf[:, :], ALU.pow).then_inc(rs_steps[kind], 1)
                pool.wait_ge(rs_steps[kind], 3 * b + 3)
                own_wait(nc.gpsimd, b)

            def double_inverse_std(f):
                k, c = "x1", 4 * f
                pool.wait_ge(mv_done[k], f + 1)
                nc.gpsimd.tensor_tensor(both[:, :], mv[k][:, :, 1], one_eps[:, :], ALU.mult).then_inc(rs_steps[k], 1)
                nc.gpsimd.tensor_tensor(negm[k][:, :], mv[k][:, :, 0], minus[:, :], ALU.mult).then_inc(rs_steps[k], 1)
                pool.wait_ge(rs_steps[k], c + 1)
                nc.gpsimd.tensor_tensor(both[:, :], both[:, :], eps_sq[:, :], ALU.add).then_inc(rs_steps[k], 1)
                pool.wait_ge(rs_steps[k], c + 3)
                nc.gpsimd.tensor_tensor(rboth[:, :], both[:, :], nhalf[:, :], ALU.pow).then_inc(rs_steps[k], 1)
                pool.wait_ge(rs_steps[k], c + 4)
                own_wait(nc.gpsimd, f)

            def single_inverse_std(f):
                nc.gpsimd.tensor_tensor(vare["x1"][:, :], mv["x1"][:, :, 1], eps[:, :], ALU.add).then_inc(rs1_steps, 1)
                pool.wait_ge(rs1_steps, 2 * f + 1)
                nc.gpsimd.tensor_tensor(rstd["x1"][:, :], vare["x1"][:, :], nhalf[:, :], ALU.pow).then_inc(rs1_steps, 1)
                pool.wait_ge(rs1_steps, 2 * f + 2)
                own_wait(nc.gpsimd, f)

            def centre_scale(dst, src, kind, scale, done, tiles=range(NT)):
                for t in tiles:
                    last = nc.gpsimd.tensor_scalar(dst[:, t, :], src[:, t, :], negm[kind][:, t:t + 1], scale[:, t:t + 1], ALU.add, ALU.mult)
                last.then_inc(done, 1)

            def add_bias(tile, done):
                last = nc.gpsimd.tensor_tensor(tile, tile, bias_bc[:, :].rearrange("p (a c) -> p a c", a=1).broadcast_to([P, NT, C]), ALU.add)
                last.then_inc(done, 1)

            def e1_states(m, h):
                pool.wait_ge(aa_done, 2 * m + h + 1)
                nc.gpsimd.tensor_tensor(z2[:, h, 0:T], e_s[:, h, 0:T], aa[:, h, 0:T], ALU.mult).then_inc(t2_done, 1)

            def norm_x_of(f, q):
                if not isinstance(f, int):
                    pool.wait_ge(turned["xa"], 2 * f - 2)
                    pool.wait_ge(r_ps, 2 * f)
                inverse_std("x", f)
                centre_scale(norm, x1[q], "x", rstd["x"], normed["x"])

            def bias_to_x(f, q):
                pool.wait_ge(normed["x"], f + 1)
                add_bias(x1[q][:, :, :], xb_done)

            def e1_sums(m):
                for h in range(CH):
                    pool.wait_ge(bb_done, 2 * m + h + 1)
                    pool.wait_ge(e_done, 2 * m + h + 1)
                    pool.wait_ge(ev_done, 2 * m + h + 1)
                    nc.gpsimd.tensor_tensor(eb_v[:, h, 0:T], e_s[:, h, 0:T], bb[:, h, 0:T], ALU.mult).then_inc(t3_done, 1)

            def den_r0(m):
                pool.wait_ge(r0_done, 2 * m + 1)
                nc.gpsimd.tensor_tensor(eb_s[:, 0, 0:T], e_v[:, 0, 0:T], eb_v[:, 0, 0:T], ALU.mult).then_inc(dr0_pool, 1)

            def norm_x1_of(f, q):
                pool.wait_ge(turned["x"], 4 if isinstance(f, int) else 2 * f + 2)
                if not isinstance(f, int):
                    pool.wait_ge(xa_done, f)
                double_inverse_std(f)
                centre_scale(norm, x1[q], "x1", rboth, normed["x1"])

            def norm_xa_of(m):
                inverse_std("xa", m)
                centre_scale(norm, xa, "xa", rstd["xa"], normed["xa"])

            def attention_sum(m, q):
                nc.gpsimd.tensor_tensor(xs[q][:, :, :], x1[q][:, :, :], xa[:, :, :], ALU.add).then_inc(xs_done, 1)

            def norm_x2_of(e, q):
                inverse_std("x2", e)
                pool.wait_ge(turned["xa"], 2 * e + 4)
                nc.gpsimd.tensor_tensor(shift_x2[:, :], negm["x2"][:, :], rstd["x2"][:, :], ALU.mult).then_inc(shift_done, 1)
                centre_scale(norm, xs[q], "x2", rstd["x2"], normed["x2"], range(TB))

            def bias_to_x2(e, q):
                pool.wait_ge(normed["x2"], e + 1)
                pool.wait_ge(normed_act, e + 1)
                add_bias(xs[q][:, :, :], x2b_done)

            def front_rests(f):
                for dst, hi, src, ready, done in ((xk_lo, xk_hi, xk, xk_hi_done, xk_lo_done), (xv_lo, xv_hi, xv, xv_hi_done, xv_lo_done)):
                    rest(nc.gpsimd, pool, dst, hi, src, ready, done, f)

            def residual_of(f, q):
                single_inverse_std(f)
                centre_scale(xa, x1[q], "x1", rstd["x1"], xa_done)

            def first_step():
                norm_x_of(0, 0)
                pool.wait_ge(s_bias, 1)
                bias_to_x(0, 0)
                pool.wait_ge(turned["x"], 2)
                norm_x_of(1, 1)
                norm_x1_of(0, 0)
                residual_of(0, 0)
                bias_to_x(1, 1)
                front_rests(0)
                pool.wait_ge(xa_done, 1)
                double_inverse_std(1)
                pool.wait_ge(turned["x1"], 2)
                centre_scale(norm, x1[1], "x1", rboth, normed["x1"])

            def second_step():
                e1_sums(0)
                e1_states(0, 0)
                e1_states(0, 1)
                den_r0(0)
                front_rests(1)
                inverse_std("xa", 0)
                pool.wait_ge(turned["x1"], 4)
                centre_scale(norm, xa, "xa", rstd["xa"], normed["xa"])
                attention_sum(0, 0)
                gate_input_rest(nc.gpsimd, pool, 0)

            def step(j, q):
                f, m, e = j, j - 1, j - 2
                norm_x_of(f, q)
                e1_sums(m)
                e1_states(m, 0)
                key_rest(nc.gpsimd, pool, e, POOL_RESTS[0])
                e1_states(m, 1)
                for n in POOL_RESTS[1:]:
                    key_rest(nc.gpsimd, pool, e, n)
                den_r0(m)
                bias_to_x(f, q)
                residual_of(m, 1 - q)
                norm_x1_of(f, q)
                inverse_std("xa", m)
                pool.wait_ge(turned["x1"], 2 * f + 2)
                own_wait(nc.gpsimd, f)
                centre_scale(norm, xa, "xa", rstd["xa"], normed["xa"])
                front_rests(f)
                norm_x2_of(e, q)
                pool.wait_ge(stored, 16 * (m - 1) + 16)
                attention_sum(m, 1 - q)
                key_input_rest(nc.gpsimd, pool, m)
                bias_to_x2(e, q)
                gate_input_rest(nc.gpsimd, pool, m)

            def last_steps(m, e):
                e1_sums(m)
                e1_states(m, 0)
                key_rest(nc.gpsimd, pool, e, POOL_RESTS[0])
                e1_states(m, 1)
                for n in POOL_RESTS[1:]:
                    key_rest(nc.gpsimd, pool, e, n)
                den_r0(m)
                residual_of(m, m % 2)
                norm_xa_of(m)
                norm_x2_of(e, e % 2)
                bias_to_x2(e, e % 2)
                pool.wait_ge(stored, 16 * (m - 1) + 16)
                attention_sum(m, m % 2)
                for n in POOL_RESTS:
                    key_rest(nc.gpsimd, pool, m, n)
                pool.wait_ge(turned["x2"], 2 * e + 2)
                for i in range(BANKS):
                    own = slice(i * TB, (i + 1) * TB)
                    pool.wait_ge(last_mv, i + 1)
                    nc.gpsimd.tensor_tensor(vare["x2"][:, own], mv["x2"][:, own, 1], eps[:, own], ALU.add).then_inc(last_steps_rs, 1)
                    nc.gpsimd.tensor_tensor(negm["x2"][:, own], mv["x2"][:, own, 0], minus[:, own], ALU.mult).then_inc(last_steps_rs, 1)
                    pool.wait_ge(last_steps_rs, 3 * i + 1)
                    nc.gpsimd.tensor_tensor(rstd["x2"][:, own], vare["x2"][:, own], nhalf[:, own], ALU.pow).then_inc(last_steps_rs, 1)
                    pool.wait_ge(last_steps_rs, 3 * i + 3)
                    nc.gpsimd.tensor_tensor(shift_x2[:, own], negm["x2"][:, own], rstd["x2"][:, own], ALU.mult).then_inc(last_shift, 1)
                    t = i * TB
                    nc.gpsimd.tensor_scalar(norm[:, t, :], xs[m % 2][:, t, :], negm["x2"][:, t:t + 1], rstd["x2"][:, t:t + 1],
                                            ALU.add, ALU.mult).then_inc(last_normed_pool, 1)
                    pool.wait_ge(last_normed_pool, i + 1)
                    pool.wait_ge(last_normed_act, i + 1)
                    nc.gpsimd.tensor_tensor(tok_bank(xs[m % 2], i), tok_bank(xs[m % 2], i),
                                            bias_bc[:, :].rearrange("p (a c) -> p a c", a=1).broadcast_to([P, TB, C]), ALU.add).then_inc(last_bias, 1)

            steps(pool, first_step, second_step, step, last_steps)


_INS = ["x", "ffn_w", "ffn_b", "ids", "gates", "vectors", "wk", "wv", "wr", "wo", "wcr", "wck", "wcv"]


def kernel(**inputs):
    import numpy as _np
    import concourse.bacc as _bacc
    from concourse import mybir as _mybir
    from concourse.bass_utils import run_bass_kernel_spmd as _run

    def given(name):
        return _np.asarray(inputs[name])

    def turned(name):
        return given(name).T

    laid = {
        "x": given("L0_attn_x"),
        "ffn_w": given("L0_ffn_W").transpose(0, 2, 1),
        "ffn_b": given("L0_ffn_b"),
        "ids": given("L0_ffn_ids"),
        "gates": given("L0_ffn_weights"),
        "vectors": _np.stack([given(f"L0_attn_{n}").reshape(-1, P) for n in VECTORS]).transpose(2, 0, 1),
        "wk": turned("L0_attn_Wk"), "wv": turned("L0_attn_Wv"), "wr": turned("L0_attn_Wr"), "wo": turned("L0_attn_Wo"),
        "wcr": turned("L0_attn_Wcr"), "wck": turned("L0_attn_Wck"), "wcv": turned("L0_attn_Wcv"),
    }
    nc = _bacc.Bacc("TRN2", target_bir_lowering=False, num_devices=1)
    arrays, args = {}, []
    for name in _INS:
        a = _np.ascontiguousarray(laid[name])
        arrays[f"in_{name}_dram"] = a
        args.append(nc.dram_tensor(f"in_{name}_dram", a.shape, _mybir.dt.from_np(a.dtype), kind="ExternalInput").ap())
    shape = laid["x"].shape
    args.append(nc.dram_tensor("out_0_dram", shape, _mybir.dt.from_np(_np.dtype("float32")), kind="ExternalOutput").ap())
    build(nc, *args)
    r = _run(nc, [arrays], core_ids=[0])
    return r.results[0]["out_0_dram"]
```
